# Optimizing a Trainium2 kernel written in Bass

```python
import numpy as np
import jax
import jax.numpy as jnp

def _softmax(x, axis=-1):
    return jax.nn.softmax(x, axis=axis)

def _gelu(x):
    return jax.nn.gelu(x, approximate=True)

def _silu(x):
    return jax.nn.silu(x)

def _sigmoid(x):
    return jax.nn.sigmoid(x)

def _layernorm(x, axis=-1, eps=1e-05):
    m = jnp.mean(x, axis=axis, keepdims=True)
    v = jnp.var(x, axis=axis, keepdims=True)
    return (x - m) / jnp.sqrt(v + eps)

def _scatter_add(tgt, idx, src, axis=0):
    return tgt.at[idx].add(src)

def _segment_sum(src, seg, n):
    return jax.ops.segment_sum(src, seg, n)
kernel_name = 'mk_decoder_postln_d2_seqx_r4_89ddae'

def setup_inputs(seed: int=0):
    np.random.seed(seed)
    _w = jnp.asarray

    def _rec_inputs():
        import jax
        import jax.numpy as jnp
        _rk = jax.random.key(seed)
        x = -0.0003929 + 0.9999 * jax.random.normal(jax.random.fold_in(_rk, 1), (16, 100, 512), jnp.float32)
        _lenS = 100 - jax.random.randint(jax.random.fold_in(_rk, 7), (16,), 0, max(1, 100 // 4) + 1, jnp.int32)
        _lenS2 = 361 - jax.random.randint(jax.random.fold_in(_rk, 8), (16,), 0, max(1, 361 // 4) + 1, jnp.int32)
        _ctx_2048P = jax.random.normal(jax.random.fold_in(_rk, 11), (16, 16, 512), jnp.float32)
        _ctx_2048c = jax.random.dirichlet(jax.random.fold_in(_rk, 511), 0.3 * jnp.ones((16,), jnp.float32), (16, 361))
        _ctx_2048t = jnp.einsum('bsk,bkd->bsd', _ctx_2048c, _ctx_2048P)
        _ctx_2048t = _ctx_2048t * jax.lax.rsqrt(jnp.mean(jnp.square(_ctx_2048t)) + 1e-12) * 0.953939
        ctx_2048 = -0.000514642 + 1.00011 * (_ctx_2048t + 0.3 * jax.random.normal(jax.random.fold_in(_rk, 611), (16, 361, 512), jnp.float32))
        _validS = jnp.arange(100)[None, :] < _lenS[:, None]
        _validS2 = jnp.arange(361)[None, :] < _lenS2[:, None]
        _causal = jnp.tril(jnp.ones((100, 100), dtype=bool))
        mask_BxS2_ik0 = jnp.where(jnp.broadcast_to(_validS2[:, :], (16, 361)), 0, 1).astype(jnp.int32)
        return (x, ctx_2048, mask_BxS2_ik0)
    x, ctx_2048, mask_BxS2_ik0 = _rec_inputs()

    def _L0_attn_setup():
        import jax, jax.numpy as jnp
        import numpy as np
        NUM_HEADS = 16

        def _l2_normalize_complex(z):
            n = jnp.sqrt(jnp.sum(jnp.abs(z) ** 2, axis=-1, keepdims=True))
            return z / n
        key = jax.random.key(seed)
        k1, k2, k3, k4 = jax.random.split(key, 4)
        B, S, D = (4, 1024, 512)
        scale = 1.0 / np.sqrt(D)
        return {'x': jax.random.normal(k1, (B, S, D), dtype=jnp.float32), 'W_q': jax.random.normal(k2, (D, D), dtype=jnp.float32) * scale, 'W_kv': jax.random.normal(k3, (D, D), dtype=jnp.float32) * scale, 'W_o': jax.random.normal(k4, (D, D), dtype=jnp.float32) * scale}
    _L0_attn_all = _L0_attn_setup()
    _L0_attn_in = {k: v for k, v in _L0_attn_all.items() if k in ('W_q', 'W_kv', 'W_o')}
    del _L0_attn_all

    def _L0_xattn_setup():
        import jax, jax.numpy as jnp
        import numpy as np
        DIM = 512
        NHEADS = 32
        HEAD_DIM = DIM // NHEADS
        EPS = 1e-06

        def _rmsnorm(t):
            return t * jax.lax.rsqrt(jnp.mean(t * t, axis=-1, keepdims=True) + EPS)
        key = jax.random.key(seed)
        kx, kc, kq, kk, kv = jax.random.split(key, 5)
        x = jax.random.normal(kx, (2, 1024, DIM), dtype=jnp.float32)
        context = jax.random.normal(kc, (2, 128, DIM), dtype=jnp.float32)
        std = 0.02
        Wq = jax.random.normal(kq, (DIM, DIM), dtype=jnp.float32) * std
        Wk = jax.random.normal(kk, (DIM, DIM), dtype=jnp.float32) * std
        Wv = jax.random.normal(kv, (DIM, DIM), dtype=jnp.float32) * std
        return {'x': x, 'context': context, 'Wq': Wq, 'Wk': Wk, 'Wv': Wv}
    _L0_xattn_all = _L0_xattn_setup()
    _L0_xattn_in = {k: v for k, v in _L0_xattn_all.items() if k in ('Wq', 'Wk', 'Wv')}
    del _L0_xattn_all

    def _L0_ffn_setup():
        import jax, jax.numpy as jnp
        import numpy as np
        NUM_ROUTED = 7
        TOP_K = 3
        D = 512
        H = 512
        B, S = (4, 512)

        def _expert_ffn(x, w1, wg, w2):
            return jax.nn.silu(x @ w1) * (x @ wg) @ w2
        key = jax.random.key(seed)
        ks = jax.random.split(key, 8)
        s = 0.02
        return {'x': jax.random.normal(ks[0], (B, S, D), jnp.float32), 'W1': jax.random.normal(ks[1], (NUM_ROUTED, D, H), jnp.float32) * s, 'Wg': jax.random.normal(ks[2], (NUM_ROUTED, D, H), jnp.float32) * s, 'W2': jax.random.normal(ks[3], (NUM_ROUTED, H, D), jnp.float32) * s, 'Ws1': jax.random.normal(ks[4], (D, H), jnp.float32) * s, 'Wsg': jax.random.normal(ks[5], (D, H), jnp.float32) * s, 'Ws2': jax.random.normal(ks[6], (H, D), jnp.float32) * s, 'gate_w': jax.random.normal(ks[7], (D, NUM_ROUTED), jnp.float32) * s, 'gate_b': jnp.zeros((NUM_ROUTED,), jnp.float32), 'biases': jnp.zeros((NUM_ROUTED,), jnp.float32)}
    _L0_ffn_all = _L0_ffn_setup()
    _L0_ffn_in = {k: v for k, v in _L0_ffn_all.items() if k in ('W1', 'Wg', 'W2', 'Ws1', 'Wsg', 'Ws2', 'gate_w', 'gate_b', 'biases')}
    del _L0_ffn_all

    def _L1_attn_setup():
        import jax, jax.numpy as jnp
        import numpy as np
        C = 512
        A = 512
        HS = 64
        H = A // HS
        DMIX = 32
        DDEC = 64
        B, T = (2, 512)
        EPS = 1e-05 * 8.0 ** 2
        key = jax.random.key(seed)
        ks = jax.random.split(key, 20)
        n = lambda i, shape, s=0.02: jax.random.normal(ks[i], shape, dtype=jnp.float32) * s
        return dict(hidden=jax.random.normal(ks[0], (B, T, C), dtype=jnp.float32), time_maa_x=n(1, (1, 1, C), 0.5), time_maa_w=n(2, (1, 1, C), 0.5), time_maa_k=n(3, (1, 1, C), 0.5), time_maa_v=n(4, (1, 1, C), 0.5), time_maa_r=n(5, (1, 1, C), 0.5), time_maa_g=n(6, (1, 1, C), 0.5), time_maa_w1=n(7, (C, DMIX * 5)), time_maa_w2=n(8, (5, DMIX, C)), time_decay=n(9, (1, 1, A), 0.5), time_decay_w1=n(10, (C, DDEC)), time_decay_w2=n(11, (DDEC, A)), time_faaaa=n(12, (H, HS), 0.5), W_r=n(13, (A, C)), W_k=n(14, (A, C)), W_v=n(15, (A, C)), W_g=n(16, (A, C)), W_o=n(17, (C, A)), ln_gamma=jnp.ones((C,), jnp.float32), ln_beta=jnp.zeros((C,), jnp.float32))
    _L1_attn_all = _L1_attn_setup()
    _L1_attn_in = {k: v for k, v in _L1_attn_all.items() if k in ('time_maa_x', 'time_maa_w', 'time_maa_k', 'time_maa_v', 'time_maa_r', 'time_maa_g', 'time_maa_w1', 'time_maa_w2', 'time_decay', 'time_decay_w1', 'time_decay_w2', 'time_faaaa', 'W_r', 'W_k', 'W_v', 'W_g', 'W_o', 'ln_gamma', 'ln_beta')}
    del _L1_attn_all

    def _L1_xattn_setup():
        import jax, jax.numpy as jnp
        import numpy as np
        import math
        H = 512
        NH = 16
        HD = H // NH
        EPS_LN = 1e-05
        RES_SCALE_MAX = 0.3

        def _nan_clean(x, lim=10000.0):
            return jnp.nan_to_num(x, nan=0.0, posinf=lim, neginf=-lim)
        key = jax.random.key(seed)
        ks = jax.random.split(key, 12)
        B, S, T = (4, 512, 64)
        std = 1.0 / math.sqrt(H)
        return {'hidden_states': jax.random.normal(ks[0], (B, S, H), jnp.float32), 'audio_tokens': jax.random.normal(ks[1], (B, T, H), jnp.float32), 'attention_mask': jax.random.randint(ks[2], (B, T), 0, 2, jnp.int32), 'Wq': jax.random.normal(ks[3], (H, H), jnp.float32) * std, 'bq': jnp.zeros((H,), jnp.float32), 'Wk': jax.random.normal(ks[4], (H, H), jnp.float32) * std, 'bk': jnp.zeros((H,), jnp.float32), 'Wv': jax.random.normal(ks[5], (H, H), jnp.float32) * std, 'bv': jnp.zeros((H,), jnp.float32), 'Wo': jax.random.normal(ks[6], (H, H), jnp.float32) * std, 'bo': jnp.zeros((H,), jnp.float32), 'ln_gamma': jnp.ones((H,), jnp.float32), 'ln_beta': jnp.zeros((H,), jnp.float32), 'residual_scale': jnp.float32(0.05)}
    _L1_xattn_all = _L1_xattn_setup()
    _L1_xattn_in = {k: v for k, v in _L1_xattn_all.items() if k in ('Wq', 'bq', 'Wk', 'bk', 'Wv', 'bv', 'Wo', 'bo', 'ln_gamma', 'ln_beta', 'residual_scale')}
    del _L1_xattn_all

    def _L1_ffn_setup():
        import jax, jax.numpy as jnp
        import numpy as np
        CAPACITY = 0.125
        HEAD_DIM = 128
        N_HEADS = 16
        N_KV_HEADS = 8
        ROPE_THETA = 10000.0
        EPS = 1e-06

        def _rms_norm(x, w):
            return x * jax.lax.rsqrt(jnp.mean(x * x, axis=-1, keepdims=True) + EPS) * w

        def _rotate_half(t):
            h = t.shape[-1] // 2
            return jnp.concatenate([-t[..., h:], t[..., :h]], axis=-1)
        key = jax.random.key(seed)
        ks = jax.random.split(key, 12)
        B, T, D = (4, 1024, 512)
        I = 2048
        s = 0.02
        return {'hidden_states': jax.random.normal(ks[0], (B, T, D), jnp.float32), 'w_router': jax.random.normal(ks[1], (D,), jnp.float32) * s, 'wq': jax.random.normal(ks[2], (D, N_HEADS * HEAD_DIM), jnp.float32) * s, 'bq': jnp.zeros((N_HEADS * HEAD_DIM,), jnp.float32), 'wk': jax.random.normal(ks[3], (D, N_KV_HEADS * HEAD_DIM), jnp.float32) * s, 'bk': jnp.zeros((N_KV_HEADS * HEAD_DIM,), jnp.float32), 'wv': jax.random.normal(ks[4], (D, N_KV_HEADS * HEAD_DIM), jnp.float32) * s, 'bv': jnp.zeros((N_KV_HEADS * HEAD_DIM,), jnp.float32), 'wo': jax.random.normal(ks[5], (N_HEADS * HEAD_DIM, D), jnp.float32) * s, 'w_gate': jax.random.normal(ks[6], (D, I), jnp.float32) * s, 'w_up': jax.random.normal(ks[7], (D, I), jnp.float32) * s, 'w_down': jax.random.normal(ks[8], (I, D), jnp.float32) * s, 'ln1_w': jnp.ones((D,), jnp.float32), 'ln2_w': jnp.ones((D,), jnp.float32)}
    _L1_ffn_all = _L1_ffn_setup()
    _L1_ffn_in = {k: v for k, v in _L1_ffn_all.items() if k in ('w_router', 'wq', 'bq', 'wk', 'bk', 'wv', 'bv', 'wo', 'w_gate', 'w_up', 'w_down', 'ln1_w', 'ln2_w')}
    del _L1_ffn_all
    return {'x': x, 'ctx_2048': ctx_2048, 'mask_BxS2_ik0': mask_BxS2_ik0, 'L0_attn_W_q': _L0_attn_in['W_q'], 'L0_attn_W_kv': _L0_attn_in['W_kv'], 'L0_attn_W_o': _L0_attn_in['W_o'], 'L0_xattn_Wq': _L0_xattn_in['Wq'], 'L0_xattn_Wk': _L0_xattn_in['Wk'], 'L0_xattn_Wv': _L0_xattn_in['Wv'], 'L0_ffn_W1': _L0_ffn_in['W1'], 'L0_ffn_Wg': _L0_ffn_in['Wg'], 'L0_ffn_W2': _L0_ffn_in['W2'], 'L0_ffn_Ws1': _L0_ffn_in['Ws1'], 'L0_ffn_Wsg': _L0_ffn_in['Wsg'], 'L0_ffn_Ws2': _L0_ffn_in['Ws2'], 'L0_ffn_gate_w': _L0_ffn_in['gate_w'], 'L0_ffn_gate_b': _L0_ffn_in['gate_b'], 'L0_ffn_biases': _L0_ffn_in['biases'], 'L1_attn_time_maa_x': _L1_attn_in['time_maa_x'], 'L1_attn_time_maa_w': _L1_attn_in['time_maa_w'], 'L1_attn_time_maa_k': _L1_attn_in['time_maa_k'], 'L1_attn_time_maa_v': _L1_attn_in['time_maa_v'], 'L1_attn_time_maa_r': _L1_attn_in['time_maa_r'], 'L1_attn_time_maa_g': _L1_attn_in['time_maa_g'], 'L1_attn_time_maa_w1': _L1_attn_in['time_maa_w1'], 'L1_attn_time_maa_w2': _L1_attn_in['time_maa_w2'], 'L1_attn_time_decay': _L1_attn_in['time_decay'], 'L1_attn_time_decay_w1': _L1_attn_in['time_decay_w1'], 'L1_attn_time_decay_w2': _L1_attn_in['time_decay_w2'], 'L1_attn_time_faaaa': _L1_attn_in['time_faaaa'], 'L1_attn_W_r': _L1_attn_in['W_r'], 'L1_attn_W_k': _L1_attn_in['W_k'], 'L1_attn_W_v': _L1_attn_in['W_v'], 'L1_attn_W_g': _L1_attn_in['W_g'], 'L1_attn_W_o': _L1_attn_in['W_o'], 'L1_attn_ln_gamma': _L1_attn_in['ln_gamma'], 'L1_attn_ln_beta': _L1_attn_in['ln_beta'], 'L1_xattn_Wq': _L1_xattn_in['Wq'], 'L1_xattn_bq': _L1_xattn_in['bq'], 'L1_xattn_Wk': _L1_xattn_in['Wk'], 'L1_xattn_bk': _L1_xattn_in['bk'], 'L1_xattn_Wv': _L1_xattn_in['Wv'], 'L1_xattn_bv': _L1_xattn_in['bv'], 'L1_xattn_Wo': _L1_xattn_in['Wo'], 'L1_xattn_bo': _L1_xattn_in['bo'], 'L1_xattn_ln_gamma': _L1_xattn_in['ln_gamma'], 'L1_xattn_ln_beta': _L1_xattn_in['ln_beta'], 'L1_xattn_residual_scale': _L1_xattn_in['residual_scale'], 'L1_ffn_w_router': _L1_ffn_in['w_router'], 'L1_ffn_wq': _L1_ffn_in['wq'], 'L1_ffn_bq': _L1_ffn_in['bq'], 'L1_ffn_wk': _L1_ffn_in['wk'], 'L1_ffn_bk': _L1_ffn_in['bk'], 'L1_ffn_wv': _L1_ffn_in['wv'], 'L1_ffn_bv': _L1_ffn_in['bv'], 'L1_ffn_wo': _L1_ffn_in['wo'], 'L1_ffn_w_gate': _L1_ffn_in['w_gate'], 'L1_ffn_w_up': _L1_ffn_in['w_up'], 'L1_ffn_w_down': _L1_ffn_in['w_down'], 'L1_ffn_ln1_w': _L1_ffn_in['ln1_w'], 'L1_ffn_ln2_w': _L1_ffn_in['ln2_w']}

def reference(x, ctx_2048, mask_BxS2_ik0, L0_attn_W_q, L0_attn_W_kv, L0_attn_W_o, L0_xattn_Wq, L0_xattn_Wk, L0_xattn_Wv, L0_ffn_W1, L0_ffn_Wg, L0_ffn_W2, L0_ffn_Ws1, L0_ffn_Wsg, L0_ffn_Ws2, L0_ffn_gate_w, L0_ffn_gate_b, L0_ffn_biases, L1_attn_time_maa_x, L1_attn_time_maa_w, L1_attn_time_maa_k, L1_attn_time_maa_v, L1_attn_time_maa_r, L1_attn_time_maa_g, L1_attn_time_maa_w1, L1_attn_time_maa_w2, L1_attn_time_decay, L1_attn_time_decay_w1, L1_attn_time_decay_w2, L1_attn_time_faaaa, L1_attn_W_r, L1_attn_W_k, L1_attn_W_v, L1_attn_W_g, L1_attn_W_o, L1_attn_ln_gamma, L1_attn_ln_beta, L1_xattn_Wq, L1_xattn_bq, L1_xattn_Wk, L1_xattn_bk, L1_xattn_Wv, L1_xattn_bv, L1_xattn_Wo, L1_xattn_bo, L1_xattn_ln_gamma, L1_xattn_ln_beta, L1_xattn_residual_scale, L1_ffn_w_router, L1_ffn_wq, L1_ffn_bq, L1_ffn_wk, L1_ffn_bk, L1_ffn_wv, L1_ffn_bv, L1_ffn_wo, L1_ffn_w_gate, L1_ffn_w_up, L1_ffn_w_down, L1_ffn_ln1_w, L1_ffn_ln2_w):
    import jax
    import jax.numpy as jnp

    def _L0_attn_ref(x, W_q, W_kv, W_o):
        import jax, jax.numpy as jnp
        import numpy as np
        NUM_HEADS = 16

        def _l2_normalize_complex(z):
            n = jnp.sqrt(jnp.sum(jnp.abs(z) ** 2, axis=-1, keepdims=True))
            return z / n
        B, S, D = x.shape
        H = NUM_HEADS
        hd = D // H
        q = (x @ W_q.T).reshape(B, S, H, hd)
        kv = (x @ W_kv.T).reshape(B, S, H, hd)
        qf = jnp.fft.fft(q, axis=-1)
        kvf = jnp.fft.fft(kv, axis=-1)
        qf = _l2_normalize_complex(qf)
        kvf = _l2_normalize_complex(kvf)
        kvf = jnp.cumsum(kvf, axis=1)
        qv = qf * kvf
        values_hat = jnp.fft.ifft(qv, axis=-1).real.astype(x.dtype)
        values_hat = values_hat.reshape(B, S, D)
        return values_hat @ W_o.T

    def _L0_xattn_ref(x, context, Wq, Wk, Wv):
        import jax, jax.numpy as jnp
        import numpy as np
        DIM = 512
        NHEADS = 32
        HEAD_DIM = DIM // NHEADS
        EPS = 1e-06

        def _rmsnorm(t):
            return t * jax.lax.rsqrt(jnp.mean(t * t, axis=-1, keepdims=True) + EPS)
        b, n, _ = x.shape
        m = context.shape[1]
        q = x @ Wq.T
        k_raw = context @ Wk.T
        v_raw = context @ Wv.T
        q = q.reshape(b, n, NHEADS, HEAD_DIM).transpose(0, 2, 1, 3)
        kv = jnp.concatenate([k_raw, v_raw], axis=-1)
        kv = kv.reshape(b, m, NHEADS, HEAD_DIM, 2)
        k = kv[..., 0].transpose(0, 2, 1, 3)
        v = kv[..., 1].transpose(0, 2, 1, 3)
        q = _rmsnorm(q)
        k = _rmsnorm(k)
        scale = HEAD_DIM ** (-0.5)
        scores = jnp.einsum('bhnd,bhmd->bhnm', q, k) * scale
        attn = jax.nn.softmax(scores, axis=-1)
        out = jnp.einsum('bhnm,bhmd->bhnd', attn, v)
        return out.transpose(0, 2, 1, 3).reshape(b, n, NHEADS * HEAD_DIM)

    def _L0_ffn_ref(x, W1, Wg, W2, Ws1, Wsg, Ws2, gate_w, gate_b, biases):
        import jax, jax.numpy as jnp
        import numpy as np
        NUM_ROUTED = 7
        TOP_K = 3
        D = 512
        H = 512
        B, S = (4, 512)

        def _expert_ffn(x, w1, wg, w2):
            return jax.nn.silu(x @ w1) * (x @ wg) @ w2
        output = _expert_ffn(x, Ws1, Wsg, Ws2)
        gate_logits = x @ gate_w + gate_b
        gate_probas = jax.nn.softmax(gate_logits, axis=-1)
        biased_probas = gate_probas + biases
        _, topk_idxs = jax.lax.top_k(biased_probas, TOP_K)
        topk_probas = jnp.take_along_axis(gate_probas, topk_idxs, axis=-1)
        topk_probas = topk_probas / jnp.sum(topk_probas, axis=-1, keepdims=True)
        for e in range(NUM_ROUTED):
            w_e = jnp.sum(topk_probas * (topk_idxs == e), axis=-1)
            output = output + _expert_ffn(x, W1[e], Wg[e], W2[e]) * w_e[..., None]
        return output

    def _L1_attn_ref(hidden, time_maa_x, time_maa_w, time_maa_k, time_maa_v, time_maa_r, time_maa_g, time_maa_w1, time_maa_w2, time_decay, time_decay_w1, time_decay_w2, time_faaaa, W_r, W_k, W_v, W_g, W_o, ln_gamma, ln_beta):
        import jax, jax.numpy as jnp
        import numpy as np
        C = 512
        A = 512
        HS = 64
        H = A // HS
        DMIX = 32
        DDEC = 64
        B, T = (2, 512)
        EPS = 1e-05 * 8.0 ** 2
        Bq, Tq, Cq = hidden.shape
        shifted = jnp.pad(hidden, ((0, 0), (1, 0), (0, 0)))[:, :-1]
        xx = shifted - hidden
        xxx = hidden + xx * time_maa_x
        z = jnp.tanh(jnp.einsum('btc,cd->btd', xxx, time_maa_w1)).reshape(Bq, Tq, 5, DMIX)
        mix = jnp.einsum('btfd,fdc->fbtc', z, time_maa_w2)
        mw, mk, mv, mr, mg = (mix[0], mix[1], mix[2], mix[3], mix[4])
        xw = hidden + xx * (time_maa_w + mw)
        xk = hidden + xx * (time_maa_k + mk)
        xv = hidden + xx * (time_maa_v + mv)
        xr = hidden + xx * (time_maa_r + mr)
        xg = hidden + xx * (time_maa_g + mg)
        r = jnp.einsum('btc,ac->bta', xr, W_r)
        k = jnp.einsum('btc,ac->bta', xk, W_k)
        v = jnp.einsum('btc,ac->bta', xv, W_v)
        g = jax.nn.silu(jnp.einsum('btc,ac->bta', xg, W_g))
        dd = jnp.einsum('btd,da->bta', jnp.tanh(jnp.einsum('btc,cd->btd', xw, time_decay_w1)), time_decay_w2) + time_decay
        w = jnp.exp(-jnp.exp(dd))
        rh = r.reshape(Bq, Tq, H, HS).transpose(1, 0, 2, 3)
        kh = k.reshape(Bq, Tq, H, HS).transpose(1, 0, 2, 3)
        vh = v.reshape(Bq, Tq, H, HS).transpose(1, 0, 2, 3)
        wh = w.reshape(Bq, Tq, H, HS).transpose(1, 0, 2, 3)
        u = time_faaaa

        def step(S, inputs):
            r_t, k_t, v_t, w_t = inputs
            kv = k_t[..., :, None] * v_t[..., None, :]
            out_t = jnp.einsum('bhn,bhnm->bhm', r_t, u[None, :, :, None] * kv + S)
            S = kv + w_t[..., :, None] * S
            return (S, out_t)
        S0 = jnp.zeros((Bq, H, HS, HS), dtype=hidden.dtype)
        _, outs = jax.lax.scan(step, S0, (rh, kh, vh, wh))
        out = outs.transpose(1, 0, 2, 3)
        mean = out.mean(-1, keepdims=True)
        var = out.var(-1, keepdims=True)
        out = (out - mean) * jax.lax.rsqrt(var + EPS)
        out = out.reshape(Bq, Tq, Cq) * ln_gamma + ln_beta
        out = out * g
        return jnp.einsum('bta,ca->btc', out, W_o)

    def _L1_xattn_ref(hidden_states, audio_tokens, attention_mask, Wq, bq, Wk, bk, Wv, bv, Wo, bo, ln_gamma, ln_beta, residual_scale):
        import jax, jax.numpy as jnp
        import numpy as np
        import math
        H = 512
        NH = 16
        HD = H // NH
        EPS_LN = 1e-05
        RES_SCALE_MAX = 0.3

        def _nan_clean(x, lim=10000.0):
            return jnp.nan_to_num(x, nan=0.0, posinf=lim, neginf=-lim)
        B, S, _ = hidden_states.shape
        T = audio_tokens.shape[1]
        hs = _nan_clean(hidden_states).astype(jnp.float32)
        at = _nan_clean(audio_tokens).astype(jnp.float32)

        def proj(x, W, b, L):
            y = x @ W.T + b
            return y.reshape(B, L, NH, HD).transpose(0, 2, 1, 3)
        q = _nan_clean(proj(hs, Wq, bq, S))
        k = _nan_clean(proj(at, Wk, bk, T))
        v = _nan_clean(proj(at, Wv, bv, T))
        scale = max(math.sqrt(HD), 1e-08)
        scores = jnp.einsum('bhsd,bhtd->bhst', q, k) / scale
        scores = jnp.clip(scores, -50.0, 50.0)
        scores = jnp.nan_to_num(scores, nan=0.0, posinf=50.0, neginf=-50.0)
        attend = (attention_mask.astype(jnp.float32) > 0.5)[:, None, None, :]
        scores = jnp.where(attend, scores, -10000.0)
        scores = jnp.clip(scores, -50.0, 50.0)
        probs = jax.nn.softmax(scores, axis=-1)
        probs = jnp.nan_to_num(probs, nan=0.0, posinf=1.0, neginf=0.0)
        probs = probs / (probs.sum(axis=-1, keepdims=True) + 1e-08)
        ctx = jnp.einsum('bhst,bhtd->bhsd', probs, v)
        ctx = ctx.transpose(0, 2, 1, 3).reshape(B, S, H)
        delta = _nan_clean(ctx @ Wo.T + bo)
        rs = jnp.clip(residual_scale, 0.0, RES_SCALE_MAX)
        delta = rs * delta
        mu = delta.mean(axis=-1, keepdims=True)
        var = jnp.mean((delta - mu) ** 2, axis=-1, keepdims=True)
        delta = (delta - mu) / jnp.sqrt(var + EPS_LN) * ln_gamma + ln_beta
        return delta

    def _L1_ffn_ref(hidden_states, w_router, wq, bq, wk, bk, wv, bv, wo, w_gate, w_up, w_down, ln1_w, ln2_w):
        import jax, jax.numpy as jnp
        import numpy as np
        CAPACITY = 0.125
        HEAD_DIM = 128
        N_HEADS = 16
        N_KV_HEADS = 8
        ROPE_THETA = 10000.0
        EPS = 1e-06

        def _rms_norm(x, w):
            return x * jax.lax.rsqrt(jnp.mean(x * x, axis=-1, keepdims=True) + EPS) * w

        def _rotate_half(t):
            h = t.shape[-1] // 2
            return jnp.concatenate([-t[..., h:], t[..., :h]], axis=-1)
        B, T, D = hidden_states.shape
        k = max(1, int(T * CAPACITY))
        scores = jnp.einsum('btd,d->bt', hidden_states, w_router)
        _, idx = jax.lax.top_k(scores, k)
        idx = jnp.sort(idx, axis=-1)
        b = jnp.arange(B)[:, None]
        sel = hidden_states[b, idx]
        sel_scores = scores[b, idx]
        S = B * k
        x = sel.reshape(S, D)
        pos = idx.reshape(S)
        inv_freq = 1.0 / ROPE_THETA ** (jnp.arange(0, HEAD_DIM, 2, dtype=jnp.float32) / HEAD_DIM)
        ang = pos.astype(jnp.float32)[:, None] * inv_freq
        cos = jnp.concatenate([jnp.cos(ang), jnp.cos(ang)], axis=-1)[:, None, :]
        sin = jnp.concatenate([jnp.sin(ang), jnp.sin(ang)], axis=-1)[:, None, :]
        h = _rms_norm(x, ln1_w)
        q = (h @ wq + bq).reshape(S, N_HEADS, HEAD_DIM)
        kk = (h @ wk + bk).reshape(S, N_KV_HEADS, HEAD_DIM)
        v = (h @ wv + bv).reshape(S, N_KV_HEADS, HEAD_DIM)
        q = q * cos + _rotate_half(q) * sin
        kk = kk * cos + _rotate_half(kk) * sin
        rep = N_HEADS // N_KV_HEADS
        kk = jnp.repeat(kk, rep, axis=1)
        v = jnp.repeat(v, rep, axis=1)
        att = jnp.einsum('shd,thd->hst', q, kk) / np.sqrt(HEAD_DIM)
        causal = jnp.tril(jnp.ones((S, S), bool))
        att = jnp.where(causal[None], att, jnp.finfo(att.dtype).min)
        att = jax.nn.softmax(att, axis=-1)
        attn_out = jnp.einsum('hst,thd->shd', att, v).reshape(S, N_HEADS * HEAD_DIM) @ wo
        x1 = x + attn_out
        h2 = _rms_norm(x1, ln2_w)
        mlp = jax.nn.silu(h2 @ w_gate) * (h2 @ w_up) @ w_down
        processed = x1 + mlp
        gate = jax.nn.sigmoid(sel_scores).reshape(S, 1)
        gated = gate * processed + (1.0 - gate) * x
        output = hidden_states.at[b, idx].set(gated.reshape(B, k, D))
        return output
    x = _layernorm(x + _L0_attn_ref(x, L0_attn_W_q, L0_attn_W_kv, L0_attn_W_o), axis=-1)
    x = _layernorm(x + _L0_xattn_ref(x, ctx_2048, L0_xattn_Wq, L0_xattn_Wk, L0_xattn_Wv), axis=-1)
    x = _layernorm(x + _L0_ffn_ref(x, L0_ffn_W1, L0_ffn_Wg, L0_ffn_W2, L0_ffn_Ws1, L0_ffn_Wsg, L0_ffn_Ws2, L0_ffn_gate_w, L0_ffn_gate_b, L0_ffn_biases), axis=-1)
    x = _layernorm(x + _L1_attn_ref(x, L1_attn_time_maa_x, L1_attn_time_maa_w, L1_attn_time_maa_k, L1_attn_time_maa_v, L1_attn_time_maa_r, L1_attn_time_maa_g, L1_attn_time_maa_w1, L1_attn_time_maa_w2, L1_attn_time_decay, L1_attn_time_decay_w1, L1_attn_time_decay_w2, L1_attn_time_faaaa, L1_attn_W_r, L1_attn_W_k, L1_attn_W_v, L1_attn_W_g, L1_attn_W_o, L1_attn_ln_gamma, L1_attn_ln_beta), axis=-1)
    x = _layernorm(x + _L1_xattn_ref(x, ctx_2048, mask_BxS2_ik0, L1_xattn_Wq, L1_xattn_bq, L1_xattn_Wk, L1_xattn_bk, L1_xattn_Wv, L1_xattn_bv, L1_xattn_Wo, L1_xattn_bo, L1_xattn_ln_gamma, L1_xattn_ln_beta, L1_xattn_residual_scale), axis=-1)
    x = _layernorm(x + _L1_ffn_ref(x, L1_ffn_w_router, L1_ffn_wq, L1_ffn_bq, L1_ffn_wk, L1_ffn_bk, L1_ffn_wv, L1_ffn_bv, L1_ffn_wo, L1_ffn_w_gate, L1_ffn_w_up, L1_ffn_w_down, L1_ffn_ln1_w, L1_ffn_ln2_w), axis=-1)
    return x

_drawn_inputs = setup_inputs


def setup_inputs(seed=0):
    import zlib

    import numpy as np

    out = dict(_drawn_inputs(seed))
    spreads = {'L0_ffn_gate_b': (0.0, 0.8),
     'L0_ffn_biases': (0.0, 0.425),
     'L1_attn_ln_gamma': (1.0, 0.6),
     'L1_attn_ln_beta': (0.0, 0.725),
     'L1_xattn_bq': (0.0, 0.1),
     'L1_xattn_bk': (0.0, 0.8),
     'L1_xattn_bv': (0.0, 0.1),
     'L1_xattn_bo': (0.0, 0.1),
     'L1_xattn_ln_gamma': (1.0, 0.2),
     'L1_xattn_ln_beta': (0.0, 0.1),
     'L1_ffn_bq': (0.0, 0.8),
     'L1_ffn_bk': (0.0, 0.8),
     'L1_ffn_bv': (0.0, 0.8),
     'L1_ffn_ln1_w': (1.0, 0.6),
     'L1_ffn_ln2_w': (1.0, 0.6)}
    factors = {'L0_ffn_gate_w': 3.506,
     'L1_attn_time_maa_x': 6.095,
     'L1_attn_time_maa_w': 8.0,
     'L1_attn_time_maa_w1': 3.599,
     'L1_attn_time_maa_w2': 3.654,
     'L1_attn_time_decay_w1': 8.0,
     'L1_attn_time_decay_w2': 8.0,
     'L1_ffn_wq': 8.0,
     'L1_ffn_wk': 8.0,
     'L1_ffn_wv': 3.309,
     'L1_ffn_wo': 2.822,
     'L1_ffn_w_gate': 4.833,
     'L1_ffn_w_up': 4.719,
     'L1_ffn_w_down': 4.715}
    for name, (base, spread) in spreads.items():
        noise = np.random.default_rng([zlib.crc32(name.encode()), seed]).standard_normal(out[name].shape)
        drawn = base * np.exp(spread * noise) if base else spread * noise
        out[name] = jnp.asarray(drawn.astype(out[name].dtype))
    for name, factor in factors.items():
        out[name] = (out[name] * factor).astype(out[name].dtype)
    return out
```

```python
from contextlib import ExitStack

import numpy as np
import concourse.bass as bass
from concourse import mybir

ALU = mybir.AluOpType
ACT = mybir.ActivationFunctionType
AX = mybir.AxisListType
F32 = mybir.dt.float32
I32 = mybir.dt.int32

B = 16
T = 100
D = 512
P = 128
C = D // P
LN_EPS = 1e-5
PAIRS = B // 2


class Chain:

    def __init__(self, eng, sem, before=0):
        self.eng, self.sem, self.n, self.base = eng, sem, before, None

    def loop(self, it, per):
        self.base, self.per, self.start = it * per, per, self.n

    def end_loop(self, trips):
        assert self.n - self.start == self.per, ("links of one iteration", self.n - self.start)
        self.n, self.base = self.start + trips * self.per, None

    def link(self, ins):
        ins.then_inc(self.sem, 1)
        self.n += 1
        return ins

    def wait(self):
        self.eng.wait_ge(self.sem, self.n if self.base is None else self.base + self.n)

    def do(self, ins):
        self.link(ins)
        self.wait()


def inv_sqrt(eng, out, in_, eps=None):
    if eps is None:
        eng.activation(out, in_, ACT.Ln)
    else:
        eng.activation(out, in_, ACT.Ln, bias=eps)
    eng.drain()
    return eng.activation(out, out, ACT.Exp, scale=-0.5)


def layer_norm(eng, y, stats, s_var, s_rstd, b):
    eng.drain()
    eng.bn_stats(stats[:, 0:6], y)
    eng.drain()
    eng.bn_aggr(stats[:, 6:8], stats[:, 0:6]).then_inc(s_var, 1)
    eng.wait_ge(s_rstd, b + 1)
    return eng.tensor_scalar(y, y, stats[:, 6:7], stats[:, 7:8], ALU.subtract, ALU.mult)


def inv_std(eng, g, v, s_var, b):
    eng.wait_ge(s_var, b + 1)
    eng.tensor_tensor(v, v, g.eps[0:T, 0:1], ALU.add)
    eng.drain()
    return eng.tensor_tensor(v, v, g.neg_half[0:T, 0:1], ALU.pow)


def stage_fft_attention(g):
    nc, PS, X, XT = g.nc, g.PS, g.X, g.XT
    with ExitStack() as st:
        sb, sem = g.in_stage(st, "fa_")
        wq_f, wkv_f, wo_f = (sb(n, [P, C, D]) for n in ("wq_f", "wkv_f", "wo_f"))
        wq_in, wkv_in, wo_in = (sb(n, [P, C, D]) for n in ("wq_in", "wkv_in", "wo_in"))
        dft, idft = sb("dft", [P, P]), sb("idft", [P, P])
        tri = sb("tri", [T, T])
        xb = sb("xb", [T, 2, D])
        xbT = sb("xbT", [P, 2, C, T])
        sq = sb("sq", [T, 2, 2, D])
        ss = sb("ss", [T, 2, 2, 16])
        qn, kn = sb("qn", [T, 2, D]), sb("kn", [T, 2, D])
        straight, cross = sb("straight", [T, 2, D]), sb("cross", [T, 2, D])
        val = sb("val", [T, 2, D])
        valT = sb("valT", [P, 2, C, T])
        y = sb("y", [T, 2, D])
        stats = sb("stats", [T, 2, 8])
        s_w, s_fold, s_foldc = sem("weights_in"), sem("folded"), sem("fold_copied")
        s_xb = [sem("x_in_even"), sem("x_in_odd")]
        s_xT, s_xTc = sem("xT_psum"), sem("xT_copied")
        s_qk, s_sq, s_ss, s_rn, s_kn = sem("qk_psum"), sem("squares"), sem("head_sums"), sem("head_norms"), sem("kn_ready")
        s_cum, s_val, s_vT, s_vTc, s_o = sem("cumsum_psum"), sem("val_ready"), sem("valT_psum"), sem("valT_copied"), sem("o_psum")
        s_var, s_rstd, s_new, s_nT, s_xsaved, s_xTsaved = (sem("var_ready"), sem("rstd_ready"), sem("x_new"), sem("newT_psum"),
                                                          sem("x_saved"), sem("xT_saved"))
        s_dve = sem("dve_chain")
        s_pool = sem("pool_chain")
        block = st.enter_context(nc.Block())

        def bank(par, n):
            return PS[:, 4 * par + n, :]

        @block.sync
        def _(eng):
            for dst, src in ((wq_in, "L0_attn_W_q"), (wkv_in, "L0_attn_W_kv"), (wo_in, "L0_attn_W_o")):
                eng.dma_start(dst[:, :, :], g.d[src].rearrange("p (c n) -> p c n", c=C)).then_inc(s_w, 16)
            eng.dma_start(dft[:, :], g.d["dft"]).then_inc(s_w, 16)
            eng.dma_start(idft[:, :], g.d["idft"]).then_inc(s_w, 16)
            eng.dma_start(tri[:, :], g.d["tri"]).then_inc(s_w, 16)
            eng.dma_start(g.ident[:, :], g.d["ident"]).then_inc(s_w, 16)
            with eng.Fori(0, PAIRS) as it:
                for par in range(2):
                    eng.wait_ge(s_xsaved, it * 2 + par + 1)
                    eng.wait_ge(s_xTsaved, it * 2 + par + 1)
                    eng.dma_start(xb[:, par, :], g.d["x"][bass.ds(it * 2 * T + par * T, T), :]).then_inc(s_xb[par], 16)

        @block.tensor
        def _(eng):
            eng.wait_ge(s_w, 16 * 7)
            n = 0
            for w_in in (wq_in, wkv_in):
                for m in range(C):
                    if n >= 2:
                        eng.wait_ge(s_foldc, n - 1)
                    for c in range(C):
                        mm = eng.matmul(PS[:, n % 2, c * P:(c + 1) * P], w_in[:, m, c * P:(c + 1) * P], dft[:, :],
                                        start=True, stop=True)
                    mm.then_inc(s_fold, 1)
                    n += 1
            for m in range(C):
                eng.wait_ge(s_foldc, n - 1)
                eng.matmul(PS[:, n % 2, :], idft[:, :], wo_in[:, m, :], start=True, stop=True).then_inc(s_fold, 1)
                n += 1
            eng.wait_ge(s_foldc, n)
            with eng.Fori(0, PAIRS) as it:
                def nth(par):
                    return it * 2 + par + 1
                for par in range(2):
                    eng.wait_ge(s_xb[par], 16 * (it + 1))
                    eng.wait_ge(s_xTsaved, nth(par))
                    for c in range(C):
                        mm = eng.transpose(bank(par, 3)[:, c * T:(c + 1) * T], xb[:, par, c * P:(c + 1) * P], g.ident[0:T, 0:T])
                    mm.then_inc(s_xT, 1)
                for par in range(2):
                    eng.wait_ge(s_xTc, nth(par))
                    for n, w in ((0, wq_f), (1, wkv_f)):
                        for c in range(C):
                            mm = eng.matmul(bank(par, n)[0:T, :], xbT[:, par, c, :], w[:, c, :], start=c == 0, stop=c == C - 1)
                    mm.then_inc(s_qk, 1)
                for par in range(2):
                    eng.wait_ge(s_kn, nth(par))
                    eng.matmul(bank(par, 2)[0:T, :], tri[:, :], kn[:, par, :], start=True, stop=True).then_inc(s_cum, 1)
                for par in range(2):
                    eng.wait_ge(s_val, nth(par))
                    for c in range(C):
                        mm = eng.transpose(bank(par, 0)[:, c * T:(c + 1) * T], val[:, par, c * P:(c + 1) * P], g.ident[0:T, 0:T])
                    mm.then_inc(s_vT, 1)
                for par in range(2):
                    eng.wait_ge(s_vTc, nth(par))
                    for c in range(C):
                        mm = eng.matmul(bank(par, 1)[0:T, :], valT[:, par, c, :], wo_f[:, c, :], start=c == 0, stop=c == C - 1)
                    mm.then_inc(s_o, 1)
                for par in range(2):
                    eng.wait_ge(s_new, nth(par))
                    for c in range(C):
                        mm = eng.transpose(bank(par, 2)[:, c * T:(c + 1) * T], y[:, par, c * P:(c + 1) * P], g.ident[0:T, 0:T])
                    mm.then_inc(s_nT, 1)

        @block.scalar
        def _(eng):
            eng.preload_act_table_set("natural_log_exp_and_others")
            n = 0
            for w_f in (wq_f, wkv_f):
                for m in range(C):
                    eng.wait_ge(s_fold, n + 1)
                    eng.activation(w_f[:, :, m * P:(m + 1) * P], PS[:, n % 2, :].rearrange("p (c n) -> p c n", c=C),
                                   ACT.Copy).then_inc(s_foldc, 1)
                    n += 1
            for m in range(C):
                eng.wait_ge(s_fold, n + 1)
                eng.activation(wo_f[:, m, :], PS[:, n % 2, :], ACT.Copy).then_inc(s_foldc, 1)
                n += 1
            with eng.Fori(0, PAIRS) as it:
                def nth(par):
                    return it * 2 + par + 1
                for par in range(2):
                    eng.wait_ge(s_xT, nth(par))
                    eng.activation(xbT[:, par, :, :].rearrange("p c t -> p (c t)"), bank(par, 3)[:, 0:C * T], ACT.Copy).then_inc(s_xTc, 1)
                for par in range(2):
                    eng.wait_ge(s_qk, nth(par))
                    eng.activation(sq[:, par, :, :], PS[0:T, 4 * par:4 * par + 2, :], ACT.Square).then_inc(s_sq, 1)
                for par in range(2):
                    eng.wait_ge(s_ss, nth(par))
                    inv_sqrt(eng, ss[:, par, :, :], ss[:, par, :, :]).then_inc(s_rn, 1)
                for par in range(2):
                    eng.wait_ge(s_vT, nth(par))
                    eng.activation(valT[:, par, :, :].rearrange("p c t -> p (c t)"), bank(par, 0)[:, 0:C * T], ACT.Copy).then_inc(s_vTc, 1)
                for par in range(2):
                    b = it * 2 + par
                    eng.wait_ge(s_nT, nth(par))
                    eng.activation(XT[:, :, bass.ds(b * T, T)], bank(par, 2)[:, 0:C * T].rearrange("p (c t) -> p c t", c=C),
                                   ACT.Copy).then_inc(s_xTsaved, 1)

        @block.vector
        def _(eng):
            ch = Chain(eng, s_dve)
            with eng.Fori(0, PAIRS) as it:
                def nth(par):
                    return it * 2 + par + 1
                ch.loop(it, 14)
                for par in range(2):
                    eng.wait_ge(s_sq, nth(par))
                    eng.tensor_reduce(ss[:, par, :, :], sq[:, par, :, :].rearrange("p a (h j) -> p a h j", j=32), AX.X, ALU.add).then_inc(s_ss, 1)
                for par in range(2):
                    eng.wait_ge(s_rn, nth(par))
                    rn = ss[:, par, :, :].unsqueeze(3)
                    eng.tensor_tensor(kn[:, par, :].rearrange("p (h j) -> p h j", j=32), bank(par, 1)[0:T, :].rearrange("p (h j) -> p h j", j=32),
                                      rn[:, 1].broadcast_to([T, 16, 32]), ALU.mult).then_inc(s_kn, 1)
                    ch.link(eng.tensor_tensor(qn[:, par, :].rearrange("p (h j) -> p h j", j=32), bank(par, 0)[0:T, :].rearrange("p (h j) -> p h j", j=32),
                                              rn[:, 0].broadcast_to([T, 16, 32]), ALU.mult))
                for par in range(2):
                    q4, k4, s4, x4, v4 = (a.rearrange("p (h s k) -> p h s k", s=2, k=16) for a in
                                          (qn[:, par, :], bank(par, 2)[0:T, :], straight[:, par, :], cross[:, par, :], val[:, par, :]))
                    eng.wait_ge(s_cum, nth(par))
                    ch.wait()
                    ch.link(eng.tensor_tensor(straight[:, par, :], qn[:, par, :], bank(par, 2)[0:T, :], ALU.mult))
                    ch.link(eng.tensor_tensor(x4[:, :, 0, :], q4[:, :, 0, :], k4[:, :, 1, :], ALU.mult))
                    ch.do(eng.tensor_tensor(x4[:, :, 1, :], q4[:, :, 1, :], k4[:, :, 0, :], ALU.mult))
                    ch.link(eng.tensor_tensor(v4[:, :, 0, :], s4[:, :, 0, :], s4[:, :, 1, :], ALU.subtract))
                    ch.do(eng.tensor_tensor(v4[:, :, 1, :], x4[:, :, 0, :], x4[:, :, 1, :], ALU.add))
                    eng.tensor_copy(v4[:, :, :, 0:1], s4[:, :, :, 0:1]).then_inc(s_val, 1)
                for par in range(2):
                    eng.wait_ge(s_o, nth(par))
                    ch.do(eng.tensor_tensor(y[:, par, :], xb[:, par, :], bank(par, 1)[0:T, :], ALU.add))
                    eng.bn_stats(stats[:, par, 0:6], y[:, par, :])
                    eng.drain()
                    eng.bn_aggr(stats[:, par, 6:8], stats[:, par, 0:6]).then_inc(s_var, 1)
                for par in range(2):
                    eng.wait_ge(s_rstd, nth(par))
                    eng.tensor_scalar(y[:, par, :], y[:, par, :], stats[:, par, 6:7], stats[:, par, 7:8], ALU.subtract, ALU.mult).then_inc(s_new, 1)
                ch.end_loop(PAIRS)

        @block.gpsimd
        def _(eng):
            eng.sem_inc(s_xsaved, 2)
            eng.sem_inc(s_xTsaved, 2)
            ch = Chain(eng, s_pool)
            ch.do(eng.memset(g.neg_half[:, :], -0.5))
            ch.do(eng.memset(g.eps[:, :], LN_EPS))
            with eng.Fori(0, PAIRS) as it:
                def nth(par):
                    return it * 2 + par + 1
                ch.loop(it, 2)
                for par in range(2):
                    eng.wait_ge(s_var, nth(par))
                    v = stats[:, par, 7:8]
                    ch.do(eng.tensor_tensor(v, v, g.eps[0:T, 0:1], ALU.add))
                    eng.tensor_tensor(v, v, g.neg_half[0:T, 0:1], ALU.pow).then_inc(s_rstd, 1)
                for par in range(2):
                    eng.wait_ge(s_new, nth(par))
                    eng.tensor_copy(X[:, bass.ds(it * 2 + par, 1), :].rearrange("p a n -> p (a n)"), y[:, par, :]).then_inc(s_xsaved, 1)
                ch.end_loop(PAIRS)


HEAD_X = 16
S2 = 361
CTX = [(0, 128), (128, 128), (256, 105)]
GROUP = 400


def stage_context_attention(g):
    nc, PS, X, XT = g.nc, g.PS, g.X, g.XT
    with ExitStack() as st:
        sb, sem = g.in_stage(st, "ca_")
        wq, wk, wv = (sb(n, [P, C, D]) for n in ("wq", "wk", "wv"))
        ones_head = sb("ones_head", [P, P])
        parity = sb("parity", [P, 2])
        eps = sb("eps", [P, 1])
        QT = sb("QT", [P, C, B * T])
        qpair = sb("qpair", [P, C, 2, T])
        ctx = sb("ctx", [P, 2, C, S2])
        KT = sb("KT", [P, C, S2])
        V = sb("V", [P, 3, 32, HEAD_X + 1])
        sq, rinv = sb("sq", [P, 2, GROUP]), sb("rinv", [P, 2, GROUP])
        E = sb("E", [P, 2, 3, 4, 2 * T])
        rsum = sb("rsum", [T, 32])
        y = sb("y", [T, 2, D])
        stats = sb("stats", [T, 2, 8])
        s_w, s_ones = sem("weights_in"), sem("ones_set")
        s_q, s_qsq, s_qss, s_qr, s_qt = sem("q_psum"), sem("q_squared"), sem("q_meansq"), sem("q_rinv"), sem("QT_ready")
        s_ctx = [sem("ctx_even"), sem("ctx_odd")]
        s_k, s_ksq, s_kss, s_kr, s_kt = sem("k_psum"), sem("k_squared"), sem("k_meansq"), sem("k_rinv"), sem("KT_ready")
        s_v, s_vc, s_qp = sem("v_psum"), sem("v_copied"), sem("qpair_ready")
        s_s, s_e, s_pv, s_read = sem("scores_psum"), sem("exp_ready"), sem("pv_psum"), sem("pv_read")
        s_var, s_rstd, s_new, s_nT, s_xsaved, s_xTsaved = (sem(n) for n in ("var", "rstd", "x_new", "newT_psum", "x_saved", "xT_saved"))
        block = st.enter_context(nc.Block())

        def ctx_rows(b):
            return g.d["ctxT"][bass.ds(b * P, P), :].rearrange("p (c n) -> p c n", c=C)

        @block.sync
        def _(eng):
            for dst, src in ((wq, "L0_xattn_Wq"), (wk, "L0_xattn_WK"), (wv, "L0_xattn_WV")):
                eng.dma_start(dst[:, :, :], g.d[src].rearrange("p (c n) -> p c n", c=C)).then_inc(s_w, 16)
            eng.dma_start(ones_head[:, :], g.d["ones_head16"]).then_inc(s_w, 16)
            eng.dma_start(parity[:, :], g.d["parity"]).then_inc(s_w, 16)
            for par in range(2):
                eng.dma_start(ctx[:, par, :, :], ctx_rows(par)).then_inc(s_ctx[par], 16)
            with eng.Fori(0, PAIRS - 1) as it:
                for par in range(2):
                    eng.wait_ge(s_s, 24 * (it * 2 + par + 1))
                    eng.dma_start(ctx[:, par, :, :], ctx_rows(it * 2 + par + 2)).then_inc(s_ctx[par], 16)

        @block.tensor
        def _(eng):
            eng.wait_ge(s_w, 16 * 5)
            with eng.Fori(0, B * T // GROUP) as it:
                def q_rows(o):
                    for c in range(C):
                        mm = eng.matmul(PS[:, o % 2, 0:GROUP], wq[:, c, o * P:(o + 1) * P], XT[:, c, bass.ds(it * GROUP, GROUP)],
                                        start=c == 0, stop=c == C - 1)
                    mm.then_inc(s_q, 1)

                def q_means(o):
                    eng.wait_ge(s_qsq, it * C + o + 1)
                    eng.matmul(PS[:, 2 + o % 2, 0:GROUP], ones_head[:, :], sq[:, o % 2, 0:GROUP], start=True, stop=True).then_inc(s_qss, 1)
                q_rows(0)
                q_rows(1)
                for o in range(C):
                    q_means(o)
                    if o + 2 < C:
                        eng.wait_ge(s_qt, it * C + o + 1)
                        q_rows(o + 2)
                eng.wait_ge(s_qt, it * C + C)

            def new_transposes(b, slot):
                eng.wait_ge(s_new, b + 1)
                for c in range(C):
                    mm = eng.transpose(PS[:, slot, c * T:(c + 1) * T], y[:, slot, c * P:(c + 1) * P], g.ident[0:T, 0:T])
                mm.then_inc(s_nT, 1)

            def pair(it, first):
                for par in range(2):
                    b = it * 2 + par

                    def k_rows(o):
                        if o >= 2:
                            eng.wait_ge(s_kt, b * C + o - 1)
                        for c in range(C):
                            mm = eng.matmul(PS[:, o % 2, 0:S2], wk[:, c, o * P:(o + 1) * P], ctx[:, par, c, :],
                                            start=c == 0, stop=c == C - 1)
                        mm.then_inc(s_k, 1)

                    def k_means(o):
                        eng.wait_ge(s_ksq, b * C + o + 1)
                        if o == 0:
                            eng.wait_ge(s_read, b + 1)
                        eng.matmul(PS[:, 2 + o % 2, 0:S2], ones_head[:, :], sq[:, o % 2, 0:S2], start=True, stop=True).then_inc(s_kss, 1)

                    def v_rows(m):
                        at, n = CTX[m]
                        for c in range(C):
                            mm = eng.matmul(PS[0:n, 4 + m, :], ctx[:, par, c, at:at + n], wv[:, c, :], start=c == 0, stop=c == C - 1)
                        mm.then_inc(s_v, 1)

                    def scores(o):
                        eng.wait_ge(s_kt, b * C + o + 1)
                        for m, (at, n) in enumerate(CTX):
                            for r in range(4):
                                u = (o * 3 + m) * 2 + r // 2
                                if u >= 2 and r % 2 == 0:
                                    eng.wait_ge(s_e, b * 24 + u - 1)
                                mm = eng.matmul(PS[0:n, 4 + r, 0:2 * T], KT[32 * r:32 * r + 32, o, at:at + n],
                                                qpair[32 * r:32 * r + 32, o, :, :].rearrange("p a t -> p (a t)"), start=True, stop=True)
                                if r % 2 == 1:
                                    mm.then_inc(s_s, 1)

                    def values(o):
                        eng.wait_ge(s_e, b * 24 + 6 * o + 6)
                        for h in range(8):
                            at = 17 * (8 * (o % 2) + h)
                            for m, (_, n) in enumerate(CTX):
                                mm = eng.matmul(PS[0:T, 2 + o // 2, at:at + 17], E[0:n, o % 2, m, h // 2, T * (h % 2):T * (h % 2) + T],
                                                V[0:n, m, 8 * o + h, :], start=m == 0, stop=m == 2)
                        if o == C - 1:
                            mm.then_inc(s_pv, 1)

                    eng.wait_ge(s_ctx[par], 16 * (it + 1))
                    if not first:
                        eng.wait_ge(s_xTsaved, b - 1)
                    k_rows(0)
                    k_rows(1)
                    v_rows(0)
                    k_means(0)
                    v_rows(1)
                    k_means(1)
                    k_rows(2)
                    v_rows(2)
                    k_rows(3)
                    k_means(2)
                    k_means(3)
                    eng.wait_ge(s_qp, b + 1)
                    eng.wait_ge(s_vc, 3 * b + 3)
                    scores(0)
                    scores(1)
                    values(0)
                    scores(2)
                    values(1)
                    scores(3)
                    if not (first and par == 0):
                        new_transposes(b - 1, 1 - par)
                    values(2)
                    values(3)
            pair(0, True)
            with eng.Fori(1, PAIRS) as it:
                pair(it, False)
            new_transposes(B - 1, 1)

        @block.scalar
        def _(eng):
            eng.preload_act_table_set("natural_log_exp_and_others")
            eng.wait_ge(s_ones, 2)
            with eng.Fori(0, B * T // GROUP) as it:
                def square(o):
                    eng.wait_ge(s_q, it * C + o + 1)
                    eng.activation(sq[:, o % 2, 0:GROUP], PS[:, o % 2, 0:GROUP], ACT.Square).then_inc(s_qsq, 1)
                square(0)
                square(1)
                for o in range(C):
                    eng.wait_ge(s_qss, it * C + o + 1)
                    inv_sqrt(eng, rinv[:, o % 2, 0:GROUP], PS[:, 2 + o % 2, 0:GROUP], eps[:, 0:1]).then_inc(s_qr, 1)
                    if o + 2 < C:
                        square(o + 2)

            def new_save(b, slot):
                eng.wait_ge(s_nT, b + 1)
                eng.activation(XT[:, :, bass.ds(b * T, T)], PS[:, slot, 0:C * T].rearrange("p (c t) -> p c t", c=C), ACT.Copy).then_inc(s_xTsaved, 1)

            def pair(it, first):
                for par in range(2):
                    b = it * 2 + par

                    def k_square(o):
                        eng.wait_ge(s_k, b * C + o + 1)
                        eng.activation(sq[:, o % 2, 0:S2], PS[:, o % 2, 0:S2], ACT.Square).then_inc(s_ksq, 1)

                    def v_copy(m):
                        n = CTX[m][1]
                        eng.wait_ge(s_v, 3 * b + m + 1)
                        eng.activation(V[0:n, m, :, 0:HEAD_X], PS[0:n, 4 + m, :].rearrange("p (h d) -> p h d", d=HEAD_X), ACT.Copy).then_inc(s_vc, 1)
                    k_square(0)
                    k_square(1)
                    for o in range(C):
                        eng.wait_ge(s_kss, b * C + o + 1)
                        inv_sqrt(eng, rinv[:, o % 2, 0:S2], PS[:, 2 + o % 2, 0:S2], eps[:, 0:1]).then_inc(s_kr, 1)
                        if o < 2:
                            v_copy(o)
                            k_square(o + 2)
                        if o == 2:
                            v_copy(2)
                    for o in range(C):
                        for m, (at, n) in enumerate(CTX):
                            for half in range(2):
                                eng.wait_ge(s_s, b * 24 + (o * 3 + m) * 2 + half + 1)
                                eng.activation(E[0:n, o % 2, m, 2 * half:2 * half + 2, :], PS[0:n, 4 + 2 * half:6 + 2 * half, 0:2 * T],
                                               ACT.Exp, scale=HEAD_X ** -0.5).then_inc(s_e, 1)
                    if not (first and par == 0):
                        new_save(b - 1, 1 - par)
            pair(0, True)
            with eng.Fori(1, PAIRS) as it:
                pair(it, False)
            new_save(B - 1, 1)

        @block.vector
        def _(eng):
            eng.memset(V[:, :, :, HEAD_X:HEAD_X + 1], 1.0).then_inc(s_ones, 1)
            eng.memset(eps[:, :], 1e-6).then_inc(s_ones, 1)
            eng.sem_inc(s_read, 1)
            with eng.Fori(0, B * T // GROUP) as it:
                for o in range(C):
                    eng.wait_ge(s_qr, it * C + o + 1)
                    eng.tensor_tensor(QT[:, o, bass.ds(it * GROUP, GROUP)], PS[:, o % 2, 0:GROUP], rinv[:, o % 2, 0:GROUP], ALU.mult).then_inc(s_qt, 1)
            eng.drain()
            with eng.Fori(0, PAIRS) as it:
                for par in range(2):
                    b = it * 2 + par
                    for j in range(2):
                        ins = eng.tensor_scalar(qpair[:, :, j, :], QT[:, :, bass.ds(b * T, T)], parity[:, j:j + 1], None, ALU.mult)
                    ins.then_inc(s_qp, 1)
                    for o in range(C):
                        eng.wait_ge(s_kr, b * C + o + 1)
                        eng.tensor_tensor(KT[:, o, :], PS[:, o % 2, 0:S2], rinv[:, o % 2, 0:S2], ALU.mult).then_inc(s_kt, 1)
                    eng.wait_ge(s_pv, b + 1)
                    o4 = PS[0:T, 2:4, 0:272].rearrange("p a (h d) -> p a h d", d=17)
                    r3 = rsum[:, :].rearrange("p (a h) -> p a h", a=2)
                    eng.tensor_copy(r3, o4[:, :, :, HEAD_X])
                    eng.drain()
                    eng.reciprocal(rsum[:, :], rsum[:, :])
                    eng.drain()
                    for a in range(2):
                        ins = eng.tensor_tensor(y[:, par, 256 * a:256 * a + 256].rearrange("p (h d) -> p h d", d=HEAD_X), o4[:, a, :, 0:HEAD_X],
                                                r3[:, a, :].unsqueeze(2).broadcast_to([T, 16, HEAD_X]), ALU.mult)
                    ins.then_inc(s_read, 1)
                    eng.drain()
                    eng.tensor_tensor(y[:, par, :], y[:, par, :], X[:, bass.ds(b, 1), :].rearrange("p a n -> p (a n)"), ALU.add)
                    layer_norm(eng, y[:, par, :], stats[:, par, :], s_var, s_rstd, b).then_inc(s_new, 1)

        @block.gpsimd
        def _(eng):
            with eng.Fori(0, PAIRS) as it:
                for par in range(2):
                    b = it * 2 + par
                    inv_std(eng, g, stats[:, par, 7:8], s_var, b).then_inc(s_rstd, 1)
                    eng.wait_ge(s_new, b + 1)
                    eng.tensor_copy(X[:, bass.ds(b, 1), :].rearrange("p a n -> p (a n)"), y[:, par, :]).then_inc(s_xsaved, 1)


EXPERTS = 8
ROUTED = EXPERTS - 1
TOP = 3
BATCHES_A_GROUP = GROUP // T


def stage_experts(g):
    nc, PS, X, XT = g.nc, g.PS, g.X, g.XT
    with ExitStack() as st:
        sb, sem = g.in_stage(st, "moe_")
        w1, wg, w2 = (sb(n, [P, 2, C, D]) for n in ("w1", "wg", "w2"))
        gate_w = sb("gate_w", [P, C, ROUTED])
        gate_b, biases = sb("gate_b", [T, ROUTED]), sb("biases", [T, ROUTED])
        earlier = sb("earlier", [T, ROUTED, ROUTED])
        logitsT = sb("logitsT", [ROUTED, B * T])
        prob, biased = sb("prob", [T, B, ROUTED]), sb("biased", [T, B, ROUTED])
        top, total = sb("top", [T, B, 1]), sb("total", [T, B, 1])
        beats, ties = sb("beats", [T, B, ROUTED * ROUTED]), sb("ties", [T, B, ROUTED * ROUTED])
        chosen = sb("chosen", [T, B, ROUTED])
        share = sb("share", [T, B, EXPERTS])
        sg = sb("sg", [P, 2, GROUP])
        aT = sb("aT", [P, 2, C, GROUP])
        y = sb("y", [T, 2, D])
        stats = sb("stats", [T, 2, 8])
        s_c = sem("gate_in")
        s_w = [sem("weights_even"), sem("weights_odd")]
        s_lg, s_lgc, s_lt, s_shift, s_exp, s_share = (sem(n) for n in ("logitsT_psum", "logitsT_copied", "logits_psum", "shifted", "exp", "share"))
        s_gu, s_sg, s_a, s_down, s_acc = sem("gate_up_psum"), sem("silu"), sem("hidden"), sem("down_psum"), sem("accumulated")
        s_var, s_rstd, s_new, s_nT, s_xsaved, s_xTsaved = (sem(n) for n in ("var", "rstd", "x_new", "newT_psum", "x_saved", "xT_saved"))
        block = st.enter_context(nc.Block())

        def load(eng, par, e):
            for dst, src in ((w1, "moe_W1"), (wg, "moe_Wg"), (w2, "moe_W2")):
                eng.dma_start(dst[:, par, :, :], g.d[src][bass.ds(e * P, P), :].rearrange("p (c n) -> p c n", c=C)).then_inc(s_w[par], 16)

        @block.sync
        def _(eng):
            for dst, src in ((gate_w, "L0_ffn_gate_w"), (gate_b, "L0_ffn_gate_b"), (biases, "L0_ffn_biases"), (earlier, "earlier")):
                d = dst[:, :] if len(dst.shape) == 2 else dst[:, :, :].rearrange("p a b -> p (a b)")
                eng.dma_start(d, g.d[src]).then_inc(s_c, 16)
            for par in range(2):
                load(eng, par, par)
            with eng.Fori(0, EXPERTS // 2 - 1) as it:
                for par in range(2):
                    eng.wait_ge(s_down, B * (it * 2 + par + 1))
                    load(eng, par, it * 2 + par + 2)

        @block.tensor
        def _(eng):
            eng.wait_ge(s_c, 16 * 4)
            for n in range(B * T // GROUP):
                for c in range(C):
                    mm = eng.matmul(PS[0:ROUTED, n, 0:GROUP], gate_w[:, c, :], XT[:, c, n * GROUP:(n + 1) * GROUP], start=c == 0, stop=c == C - 1)
                mm.then_inc(s_lg, 1)
            eng.wait_ge(s_lgc, B * T // GROUP)
            for b in range(B):
                mm = eng.transpose(PS[0:T, 4, b * ROUTED:(b + 1) * ROUTED], logitsT[:, b * T:(b + 1) * T], g.ident[0:ROUTED, 0:ROUTED])
            mm.then_inc(s_lt, 1)
            eng.wait_ge(s_shift, 1)
            with eng.Fori(0, EXPERTS // 2) as it:
                for par in range(2):
                    e = it * 2 + par

                    def up(t):
                        for h in range(C):
                            n = t * C + h
                            eng.wait_ge(s_a, e * 16 + n + 1)
                            for k, w in ((0, wg), (2, w1)):
                                for c in range(C):
                                    mm = eng.matmul(PS[:, k + n % 2, 0:GROUP], w[:, par, c, h * P:(h + 1) * P], XT[:, c, t * GROUP:(t + 1) * GROUP],
                                                    start=c == 0, stop=c == C - 1)
                            mm.then_inc(s_gu, 1)

                    def down(t):
                        eng.wait_ge(s_a, e * 16 + 2 + 4 * t + 4)
                        for i in range(BATCHES_A_GROUP):
                            b = t * BATCHES_A_GROUP + i
                            eng.wait_ge(s_acc, e * B + b + 1)
                            for h in range(C):
                                mm = eng.matmul(PS[0:T, 4 + i, :], aT[:, t % 2, h, i * T:(i + 1) * T], w2[:, par, h, :], start=h == 0, stop=h == C - 1)
                            mm.then_inc(s_down, 1)
                    eng.wait_ge(s_w[par], 48 * (it + 1))
                    up(0)
                    up(1)
                    down(0)
                    up(2)
                    down(1)
                    up(3)
                    down(2)
                    down(3)
            with eng.Fori(0, PAIRS) as it:
                for par in range(2):
                    b = it * 2 + par
                    eng.wait_ge(s_new, b + 1)
                    eng.wait_ge(s_xTsaved, b + 1)
                    for c in range(C):
                        mm = eng.transpose(PS[:, par, c * T:(c + 1) * T], y[:, par, c * P:(c + 1) * P], g.ident[0:T, 0:T])
                    mm.then_inc(s_nT, 1)

        @block.scalar
        def _(eng):
            for n in range(B * T // GROUP):
                eng.wait_ge(s_lg, n + 1)
                eng.activation(logitsT[:, n * GROUP:(n + 1) * GROUP], PS[0:ROUTED, n, 0:GROUP], ACT.Copy).then_inc(s_lgc, 1)
            eng.wait_ge(s_shift, 1)
            eng.activation(prob[:, :, :], prob[:, :, :], ACT.Exp).then_inc(s_exp, 1)
            with eng.Fori(0, EXPERTS) as e:
                for n in range(16):
                    eng.wait_ge(s_gu, e * 16 + n + 1)
                    eng.activation(sg[:, n % 2, :], PS[:, 2 + n % 2, 0:GROUP], ACT.Silu).then_inc(s_sg, 1)
            with eng.Fori(0, PAIRS) as it:
                for par in range(2):
                    b = it * 2 + par
                    eng.wait_ge(s_nT, b + 1)
                    eng.activation(XT[:, :, bass.ds(b * T, T)], PS[:, par, 0:C * T].rearrange("p (c t) -> p c t", c=C), ACT.Copy).then_inc(s_xTsaved, 1)

        @block.vector
        def _(eng):
            eng.sem_inc(s_a, 2)
            eng.sem_inc(s_acc, 4)
            eng.wait_ge(s_c, 16 * 4)
            eng.wait_ge(s_lt, 1)
            per_batch = [T, B, ROUTED]
            eng.tensor_tensor(prob[:, :, :], PS[0:T, 4, 0:B * ROUTED].rearrange("p (b e) -> p b e", e=ROUTED),
                              gate_b[:, :].unsqueeze(1).broadcast_to(per_batch), ALU.add)
            eng.drain()
            eng.tensor_reduce(top[:, :, 0], prob[:, :, :], AX.X, ALU.max)
            eng.drain()
            eng.tensor_tensor(prob[:, :, :], prob[:, :, :], top[:, :, :].broadcast_to(per_batch), ALU.subtract).then_inc(s_shift, 1)
            eng.wait_ge(s_exp, 1)
            eng.tensor_reduce(total[:, :, 0], prob[:, :, :], AX.X, ALU.add)
            eng.drain()
            eng.reciprocal(total[:, :, :], total[:, :, :])
            eng.drain()
            eng.tensor_tensor(prob[:, :, :], prob[:, :, :], total[:, :, :].broadcast_to(per_batch), ALU.mult)
            eng.drain()
            eng.tensor_tensor(biased[:, :, :], prob[:, :, :], biases[:, :].unsqueeze(1).broadcast_to(per_batch), ALU.add)
            eng.drain()
            e4, j4 = biased[:, :, :].unsqueeze(3), biased[:, :, :].unsqueeze(2)
            pair = [T, B, ROUTED, ROUTED]
            b4, t4 = (a[:, :, :].rearrange("p b (e j) -> p b e j", j=ROUTED) for a in (beats, ties))
            eng.tensor_tensor(b4, j4.broadcast_to(pair), e4.broadcast_to(pair), ALU.is_gt)
            eng.tensor_tensor(t4, j4.broadcast_to(pair), e4.broadcast_to(pair), ALU.is_equal)
            eng.drain()
            eng.tensor_tensor(ties[:, :, :], ties[:, :, :], earlier[:, :, :].rearrange("p e j -> p (e j)").unsqueeze(1).broadcast_to([T, B, ROUTED * ROUTED]), ALU.mult)
            eng.drain()
            eng.tensor_tensor(beats[:, :, :], beats[:, :, :], ties[:, :, :], ALU.add)
            eng.drain()
            eng.tensor_reduce(chosen[:, :, :], b4, AX.X, ALU.add)
            eng.drain()
            eng.tensor_scalar(chosen[:, :, :], chosen[:, :, :], TOP - 0.5, None, ALU.is_lt)
            eng.drain()
            eng.tensor_tensor(prob[:, :, :], prob[:, :, :], chosen[:, :, :], ALU.mult)
            eng.drain()
            eng.tensor_reduce(total[:, :, 0], prob[:, :, :], AX.X, ALU.add)
            eng.drain()
            eng.reciprocal(total[:, :, :], total[:, :, :])
            eng.memset(share[:, :, 0:1], 1.0)
            eng.drain()
            eng.tensor_tensor(share[:, :, 1:EXPERTS], prob[:, :, :], total[:, :, :].broadcast_to(per_batch), ALU.mult)
            eng.drain()
            with eng.Fori(0, EXPERTS) as e:
                def hidden(t):
                    for h in range(C):
                        n = t * C + h
                        eng.wait_ge(s_sg, e * 16 + n + 1)
                        eng.tensor_tensor(aT[:, t % 2, h, :], PS[:, n % 2, 0:GROUP], sg[:, n % 2, :], ALU.mult).then_inc(s_a, 1)

                def accumulate(t):
                    for i in range(BATCHES_A_GROUP):
                        b = t * BATCHES_A_GROUP + i
                        eng.wait_ge(s_down, e * B + b + 1)
                        eng.scalar_tensor_tensor(X[:, b, :], PS[0:T, 4 + i, :], share[:, b, bass.ds(e, 1)], X[:, b, :], ALU.mult, ALU.add).then_inc(s_acc, 1)
                hidden(0)
                hidden(1)
                accumulate(0)
                hidden(2)
                accumulate(1)
                hidden(3)
                accumulate(2)
                accumulate(3)
            eng.drain()
            eng.sem_inc(s_xsaved, 2)
            eng.sem_inc(s_xTsaved, 2)
            with eng.Fori(0, PAIRS) as it:
                for par in range(2):
                    b = it * 2 + par
                    eng.wait_ge(s_xsaved, b + 1)
                    eng.wait_ge(s_xTsaved, b + 1)
                    eng.tensor_copy(y[:, par, :], X[:, bass.ds(b, 1), :].rearrange("p a n -> p (a n)"))
                    layer_norm(eng, y[:, par, :], stats[:, par, :], s_var, s_rstd, b).then_inc(s_new, 1)

        @block.gpsimd
        def _(eng):
            with eng.Fori(0, PAIRS) as it:
                for par in range(2):
                    b = it * 2 + par
                    inv_std(eng, g, stats[:, par, 7:8], s_var, b).then_inc(s_rstd, 1)
                    eng.wait_ge(s_new, b + 1)
                    eng.tensor_copy(X[:, bass.ds(b, 1), :].rearrange("p a n -> p (a n)"), y[:, par, :]).then_inc(s_xsaved, 1)


HEADS_R, HEAD_R = 8, 64
LEVELS = 7
PAD = 1 << LEVELS
MIX = 32
MIXES = ("w", "k", "v", "r", "g")
GN_EPS = 1e-5 * 8.0 ** 2


def stage_recurrence(g):
    nc, PS, X, XT = g.nc, g.PS, g.X, g.XT
    with ExitStack() as st:
        sb, sem = g.in_stage(st, "rec_")
        wt = {n: sb("w_" + n, [P, C, D]) for n in "rkvgo"}
        maa_w1 = sb("maa_w1", [P, C, 5 * MIX])
        maa_w2, maa_w2g = sb("maa_w2", [P, D]), sb("maa_w2g", [MIX, D])
        dec_w1, dec_w2 = sb("dec_w1", [P, C, HEAD_R]), sb("dec_w2", [HEAD_R, D])
        cols = sb("cols", [P, 8, C])
        gamma, beta = sb("gamma", [T, D]), sb("beta", [T, D])
        mask = sb("mask", [T, 8, T])
        work = sb("work", [P, 4 * C * GROUP])
        xs, xx, xf0, xf1 = (work[:, n * C * GROUP:(n + 1) * C * GROUP].rearrange("p (c n) -> p c n", c=C) for n in range(4))
        XL = work[:, 0:8 * C * PAD].rearrange("p (l c t) -> p l c t", l=8, c=C)
        Pre, Suf = (work[:, (8 + n) * C * PAD:(9 + n) * C * PAD].rearrange("p (c t) -> p c t", c=C) for n in range(2))
        tot = sb("tot", [P, 2, C, 32])
        z, zg = sb("z", [P, GROUP]), sb("zg", [MIX, GROUP])
        tw = sb("tw", [HEAD_R, GROUP])
        ew = sb("ew", [P, GROUP])
        R, K, W = (sb(n, [P, C, BATCHES_A_GROUP, PAD]) for n in ("R", "K", "W"))
        V, G = sb("V", [T, BATCHES_A_GROUP, D]), sb("G", [T, BATCHES_A_GROUP, D])
        th = sb("th", [T, 2, D])
        GM = sb("GM", [T, 2, 8, T])
        mean, var = sb("mean", [T, 8, 1]), sb("var", [T, 8, 1])
        o, sq = sb("o", [T, D]), sb("sq", [T, D])
        oT = sb("oT", [P, C, T])
        y = sb("y", [T, 2, D])
        stats = sb("stats", [T, 2, 8])
        s_w, s_init = sem("small_weights_in"), sem("pads_set")
        s_wt = {n: sem("w_" + n + "_in") for n in "rkvgo"}
        s_xs, s_xxx, s_z, s_tz = sem("x_staged"), sem("xxx"), sem("z_psum"), sem("z_tanh")
        s_mix, s_t1, s_xf = sem("mix_psum"), sem("mix_taken"), sem("xf_ready")
        s_wd, s_tw, s_pr, s_ev, s_th, s_g = sem("decay_psum"), sem("decay_tanh"), sem("proj_psum"), sem("proj_taken"), sem("gate_tanh"), sem("gate_ready")
        s_xr, s_xk = sem("r_levels"), sem("k_levels")
        s_gp, s_gm, s_o = sem("pairs_psum"), sem("pairs_masked"), sem("out_psum")
        s_cent, s_sq, s_var, s_gr, s_og, s_oT, s_oTc, s_wo = (sem(n) for n in ("centred", "centred_sq", "head_var", "head_rstd", "gated", "oT_psum", "oT_copied", "wo_psum"))
        s_xvar, s_rstd, s_new, s_nT, s_xsaved, s_xTsaved = (sem(n) for n in ("var", "rstd", "x_new", "newT_psum", "x_saved", "xT_saved"))
        block = st.enter_context(nc.Block())
        NB = BATCHES_A_GROUP

        def half(a, h, side):
            return a.rearrange("p c (s two h) -> p c s two h", two=2, h=h)[:, :, :, side, :]

        @block.sync
        def _(eng):
            for dst, src in ((maa_w1, "L1_attn_time_maa_w1"), (maa_w2, "maa_w2"), (maa_w2g, "maa_w2g"), (dec_w1, "L1_attn_time_decay_w1"),
                             (dec_w2, "L1_attn_time_decay_w2"), (cols, "rec_cols"), (gamma, "L1_attn_ln_gamma"), (beta, "L1_attn_ln_beta"), (mask, "pair_mask")):
                d = dst[:, :] if len(dst.shape) == 2 else dst[:, :, :].rearrange("p a b -> p (a b)")
                eng.dma_start(d, g.d[src]).then_inc(s_w, 16)
            for n in (*MIXES[1:], "o"):
                eng.dma_start(wt[n][:, :, :], g.d["L1_attn_W_" + n].rearrange("p (c n) -> p c n", c=C)).then_inc(s_wt[n], 16)

        @block.tensor
        def _(eng):
            eng.wait_ge(s_w, 16 * 9)
            with eng.Fori(0, B // NB) as gi:
                def mixes(f):
                    w2 = maa_w2[32 * f:32 * f + 32, :] if f < 4 else maa_w2g[:, :]
                    zf = z[32 * f:32 * f + 32, :] if f < 4 else zg[:, :]
                    for c in range(C):
                        m = f * C + c
                        if m >= 2:
                            eng.wait_ge(s_t1, gi * 20 + m - 1)
                        eng.matmul(PS[:, m % 2, 0:GROUP], w2[:, c * P:(c + 1) * P], zf, start=True, stop=True).then_inc(s_mix, 1)

                def projection(f):
                    name = MIXES[f]
                    xf = (xf0, xf1)[(f + 1) % 2]
                    eng.wait_ge(s_xf, gi * 20 + 4 * f + 4)
                    if name == "w":
                        for c in range(C):
                            mm = eng.matmul(PS[0:HEAD_R, 2, 0:GROUP], dec_w1[:, c, :], xf[:, c, :], start=c == 0, stop=c == C - 1)
                        mm.then_inc(s_wd, 1)
                        eng.wait_ge(s_tw, gi + 1)
                    else:
                        eng.wait_ge(s_wt[name], 16)
                    for i in range(4):
                        u = f * 4 + i
                        if f >= 1:
                            eng.wait_ge(s_ev, gi * 16 + u - 3)
                        if name == "w":
                            mm = eng.matmul(PS[:, 4 + i, 0:GROUP], dec_w2[:, i * P:(i + 1) * P], tw[:, :], start=True, stop=True)
                        else:
                            for c in range(C):
                                if name in "kr":
                                    mm = eng.matmul(PS[:, 4 + i, 0:GROUP], wt[name][:, c, i * P:(i + 1) * P], xf[:, c, :], start=c == 0, stop=c == C - 1)
                                else:
                                    mm = eng.matmul(PS[0:T, 4 + i, :], xf[:, c, i * T:(i + 1) * T], wt[name][:, c, :], start=c == 0, stop=c == C - 1)
                        mm.then_inc(s_pr, 1)

                eng.wait_ge(s_xxx, gi + 1)
                for c in range(C):
                    eng.matmul(PS[:, 0, 0:GROUP], maa_w1[:, c, 0:P], xf0[:, c, :], start=c == 0, stop=c == C - 1)
                for c in range(C):
                    mm = eng.matmul(PS[0:MIX, 1, 0:GROUP], maa_w1[:, c, P:P + MIX], xf0[:, c, :], start=c == 0, stop=c == C - 1)
                mm.then_inc(s_z, 1)
                eng.wait_ge(s_tz, gi + 1)
                mixes(0)
                for f in range(5):
                    if f < 4:
                        mixes(f + 1)
                    projection(f)
                eng.wait_ge(s_g, gi * NB + NB)

                def pairs(i, k):
                    n = (gi * NB + i) * 8 + k
                    at = slice(64 * (k % 2), 64 * (k % 2) + 64)
                    if k % 4 == 0:
                        eng.wait_ge(s_xr, (gi * NB + i) * 2 + k // 4 + 1)
                        eng.wait_ge(s_xk, (gi * NB + i) * 2 + k // 4 + 1)
                    if i > 0 or k >= 2:
                        eng.wait_ge(s_gm, n - 1)
                    for l in range(8):
                        rhs = XL[at, l, k // 2, 0:T] if l < LEVELS else R[at, k // 2, i, 0:T]
                        mm = eng.matmul(PS[0:T, 2 * (k % 2) + l // 4, (l % 4) * T:(l % 4 + 1) * T], XL[at, l, k // 2, 0:T], rhs, start=True, stop=True)
                    mm.then_inc(s_gp, 1)

                def head_out(i, k):
                    eng.wait_ge(s_gm, (gi * NB + i) * 8 + k + 1)
                    for l in range(8):
                        mm = eng.matmul(PS[0:T, 4 + i % 2, k * HEAD_R:(k + 1) * HEAD_R], GM[:, k % 2, l, :], V[:, i, k * HEAD_R:(k + 1) * HEAD_R],
                                        start=l == 0, stop=l == 7)
                    if k == 7:
                        mm.then_inc(s_o, 1)

                def out_transposes(i):
                    eng.wait_ge(s_og, gi * NB + i + 1)
                    if i > 0:
                        eng.wait_ge(s_xTsaved, gi * NB + i)
                    for c in range(C):
                        mm = eng.transpose(PS[:, 7, c * T:(c + 1) * T], o[:, c * P:(c + 1) * P], g.ident[0:T, 0:T])
                    mm.then_inc(s_oT, 1)

                def project(i):
                    eng.wait_ge(s_oTc, gi * NB + i + 1)
                    eng.wait_ge(s_wt["o"], 16)
                    for c in range(C):
                        mm = eng.matmul(PS[0:T, 6, :], oT[:, c, :], wt["o"][:, c, :], start=c == 0, stop=c == C - 1)
                    mm.then_inc(s_wo, 1)

                def new_transposes(i):
                    eng.wait_ge(s_new, gi * NB + i + 1)
                    for c in range(C):
                        mm = eng.transpose(PS[:, 7, c * T:(c + 1) * T], y[:, i % 2, c * P:(c + 1) * P], g.ident[0:T, 0:T])
                    mm.then_inc(s_nT, 1)

                pairs(0, 0)
                for i in range(NB):
                    for k in range(8):
                        if k < 7:
                            pairs(i, k + 1)
                        elif i < NB - 1:
                            pairs(i + 1, 0)
                        head_out(i, k)
                        if i > 0 and k == 5:
                            out_transposes(i - 1)
                        if i > 0 and k == 6:
                            project(i - 1)
                    if i > 0:
                        new_transposes(i - 1)
                out_transposes(NB - 1)
                project(NB - 1)
                new_transposes(NB - 1)
                eng.wait_ge(s_xTsaved, gi * NB + NB)

        @block.scalar
        def _(eng):
            eng.wait_ge(s_w, 16 * 9)
            eng.wait_ge(s_init, 3)
            with eng.Fori(0, B // NB) as gi:
                eng.wait_ge(s_z, gi + 1)
                eng.activation(z[:, :], PS[:, 0, 0:GROUP], ACT.Tanh)
                eng.activation(zg[:, :], PS[0:MIX, 1, 0:GROUP], ACT.Tanh).then_inc(s_tz, 1)
                for f, name in enumerate(MIXES):
                    if name == "w":
                        eng.wait_ge(s_wd, gi + 1)
                        eng.activation(tw[:, :], PS[0:HEAD_R, 2, 0:GROUP], ACT.Tanh).then_inc(s_tw, 1)
                    for i in range(4):
                        eng.wait_ge(s_pr, gi * 20 + f * 4 + i + 1)
                        by_batch = PS[:, 4 + i, 0:GROUP].rearrange("p (b t) -> p b t", t=T)
                        if name == "w":
                            eng.activation(ew[:, :], PS[:, 4 + i, 0:GROUP], ACT.Exp, bias=cols[:, 6, i:i + 1])
                            eng.drain()
                            eng.activation(W[:, i, :, 0:T], ew[:, :].rearrange("p (b t) -> p b t", t=T), ACT.Exp, scale=-1.0).then_inc(s_ev, 1)
                            eng.drain()
                        elif name in "kr":
                            eng.activation({"k": K, "r": R}[name][:, i, :, 0:T], by_batch, ACT.Copy).then_inc(s_ev, 1)
                        elif name == "v":
                            eng.activation(V[:, i, :], PS[0:T, 4 + i, :], ACT.Copy).then_inc(s_ev, 1)
                        else:
                            if i >= 2:
                                eng.wait_ge(s_g, gi * NB + i - 1)
                            eng.activation(th[:, i % 2, :], PS[0:T, 4 + i, :], ACT.Tanh, scale=0.5).then_inc(s_th, 1)
                for i in range(NB):
                    b = gi * NB + i
                    eng.wait_ge(s_cent, b + 1)
                    eng.activation(sq[:, :], o[:, :], ACT.Square).then_inc(s_sq, 1)
                    eng.wait_ge(s_oT, b + 1)
                    eng.activation(oT[:, :, :], PS[:, 7, 0:C * T].rearrange("p (c t) -> p c t", c=C), ACT.Copy).then_inc(s_oTc, 1)
                    eng.wait_ge(s_nT, b + 1)
                    eng.activation(XT[:, :, bass.ds(b * T, T)], PS[:, 7, 0:C * T].rearrange("p (c t) -> p c t", c=C), ACT.Copy).then_inc(s_xTsaved, 1)

        @block.vector
        def _(eng):
            eng.memset(R[:, :, :, :], 0.0).then_inc(s_init, 1)
            eng.memset(K[:, :, :, :], 0.0).then_inc(s_init, 1)
            eng.memset(W[:, :, :, :], 1.0).then_inc(s_init, 1)
            eng.wait_ge(s_w, 16 * 9)
            with eng.Fori(0, B // NB) as gi:
                eng.wait_ge(s_xs, gi + 1)
                xs3, xx3 = (a.rearrange("p c (b t) -> p (c b) t", t=T) for a in (xs, xx))
                eng.tensor_tensor(xx3[:, :, 1:T], xs3[:, :, 0:T - 1], xs3[:, :, 1:T], ALU.subtract)
                eng.tensor_scalar(xx3[:, :, 0:1], xs3[:, :, 0:1], -1.0, None, ALU.mult)
                eng.drain()
                for c in range(C):
                    ins = eng.scalar_tensor_tensor(xf0[:, c, :], xx[:, c, :], cols[:, 0, c:c + 1], xs[:, c, :], ALU.mult, ALU.add)
                ins.then_inc(s_xxx, 1)
                for f in range(5):
                    for c in range(C):
                        m = f * C + c
                        eng.wait_ge(s_mix, gi * 20 + m + 1)
                        eng.scalar_tensor_tensor((xf0, xf1)[(f + 1) % 2][:, c, :], PS[:, m % 2, 0:GROUP], cols[:, 1 + f, c:c + 1], xx[:, c, :],
                                                 ALU.add, ALU.mult).then_inc(s_t1, 1)
                for i in range(NB):
                    eng.wait_ge(s_th, gi * NB + i + 1)
                    eng.scalar_tensor_tensor(G[:, i, :], th[:, i % 2, :], 1.0, PS[0:T, 4 + i, :], ALU.add, ALU.mult).then_inc(s_g, 1)
                eng.wait_ge(s_ev, gi * 16 + 16)

                def right_levels(i, part, levels):
                    two = slice(2 * part, 2 * part + 2)
                    r, w, pre = R[:, two, i, :], W[:, two, i, :], Pre[:, two]
                    for l in levels:
                        h = 1 << l
                        if l == 0:
                            eng.tensor_copy(half(XL[:, 0, two], 1, 1), half(r, 1, 1))
                            eng.memset(half(pre, 1, 0), 1.0)
                            eng.tensor_copy(half(pre, 1, 1), half(w, 1, 0))
                            continue
                        eng.drain()
                        ins = eng.tensor_tensor(half(XL[:, l, two], h, 1), half(r, h, 1), half(pre, h, 1), ALU.mult)
                        if l < LEVELS - 1:
                            left = tot[:, 0, two, 0:PAD // (2 * h)]
                            eng.tensor_tensor(left, half(pre, h, 0)[:, :, :, h - 1], half(w, h, 0)[:, :, :, h - 1], ALU.mult)
                            eng.drain()
                            eng.tensor_tensor(half(pre, h, 1), half(pre, h, 1), left.unsqueeze(3).broadcast_to([P, 2, PAD // (2 * h), h]), ALU.mult)
                        else:
                            ins.then_inc(s_xr, 1)

                by_head = [T, HEADS_R, HEAD_R]
                o3, sq3 = (a.rearrange("p (h m) -> p h m", m=HEAD_R) for a in (o[:, :], sq[:, :]))

                def centre(i):
                    ps3 = PS[0:T, 4 + i % 2, :].rearrange("p (h m) -> p h m", m=HEAD_R)
                    eng.wait_ge(s_o, gi * NB + i + 1)
                    eng.tensor_reduce(mean[:, :, 0], ps3, AX.X, ALU.add)
                    eng.drain()
                    eng.tensor_scalar(mean[:, :, :], mean[:, :, :], 1.0 / HEAD_R, None, ALU.mult)
                    eng.drain()
                    eng.tensor_tensor(o3, ps3, mean[:, :, :].broadcast_to(by_head), ALU.subtract).then_inc(s_cent, 1)

                def head_variance(i):
                    eng.wait_ge(s_sq, gi * NB + i + 1)
                    eng.tensor_reduce(var[:, :, 0], sq3, AX.X, ALU.add)
                    eng.drain()
                    eng.tensor_scalar(var[:, :, 0], var[:, :, 0], 1.0 / HEAD_R, GN_EPS, ALU.mult, ALU.add).then_inc(s_var, 1)

                def gate(i):
                    eng.wait_ge(s_gr, gi * NB + i + 1)
                    eng.tensor_tensor(o3, o3, var[:, :, :].broadcast_to(by_head), ALU.mult)
                    eng.drain()
                    eng.tensor_tensor(o[:, :], o[:, :], gamma[:, :], ALU.mult)
                    eng.drain()
                    eng.tensor_tensor(o[:, :], o[:, :], beta[:, :], ALU.add)
                    eng.drain()
                    eng.scalar_tensor_tensor(o[:, :], o[:, :], 0.5, G[:, i, :], ALU.mult, ALU.mult).then_inc(s_og, 1)

                def residual_norm(i):
                    b = gi * NB + i
                    eng.wait_ge(s_wo, b + 1)
                    eng.tensor_tensor(y[:, i % 2, :], PS[0:T, 6, :], X[:, bass.ds(b, 1), :].rearrange("p a n -> p (a n)"), ALU.add)
                    layer_norm(eng, y[:, i % 2, :], stats[:, i % 2, :], s_xvar, s_rstd, b).then_inc(s_new, 1)

                right_levels(0, 0, range(LEVELS))
                for i in range(NB):
                    for k in range(8):
                        eng.wait_ge(s_gp, (gi * NB + i) * 8 + k + 1)
                        eng.tensor_tensor(GM[:, k % 2, :, :].rearrange("p (a l) t -> p a (l t)", a=2), PS[0:T, 2 * (k % 2):2 * (k % 2) + 2, 0:4 * T],
                                          mask[:, :, :].rearrange("p (a l) t -> p a (l t)", a=2), ALU.mult).then_inc(s_gm, 1)
                        if k == 0:
                            right_levels(i, 1, range(0, 4))
                        if k == 1:
                            right_levels(i, 1, range(4, LEVELS))
                        if k == 2 and i > 0:
                            centre(i - 1)
                        if k == 3 and i > 0:
                            head_variance(i - 1)
                        if k == 3 and i < NB - 1:
                            right_levels(i + 1, 0, range(0, 3))
                        if k == 4 and i > 0:
                            gate(i - 1)
                        if k == 5 and i < NB - 1:
                            right_levels(i + 1, 0, range(3, LEVELS))
                        if k == 7 and i > 0:
                            residual_norm(i - 1)
                centre(NB - 1)
                head_variance(NB - 1)
                gate(NB - 1)
                residual_norm(NB - 1)

        @block.gpsimd
        def _(eng):
            eng.wait_ge(s_w, 16 * 9)
            with eng.Fori(0, B // NB) as gi:
                eng.tensor_copy(xs, XT[:, :, bass.ds(gi * GROUP, GROUP)]).then_inc(s_xs, 1)
                for f in range(5):
                    for c in range(C):
                        eng.wait_ge(s_t1, gi * 20 + f * C + c + 1)
                        xf = (xf0, xf1)[(f + 1) % 2][:, c, :]
                        eng.tensor_tensor(xf, xf, xs[:, c, :], ALU.add).then_inc(s_xf, 1)
                eng.wait_ge(s_g, gi * NB + NB)
                eng.wait_ge(s_ev, gi * 16 + 16)

                def left_levels(i, part):
                    two = slice(2 * part, 2 * part + 2)
                    k, w, suf = K[:, two, i, :], W[:, two, i, :], Suf[:, two]
                    eng.tensor_tensor(XL[:, 7, two], k, cols[:, 7, two].unsqueeze(2).broadcast_to([P, 2, PAD]), ALU.mult)
                    eng.tensor_copy(half(XL[:, 0, two], 1, 0), half(k, 1, 0))
                    eng.memset(half(suf, 1, 1), 1.0)
                    eng.tensor_copy(half(suf, 1, 0), half(w, 1, 1))
                    for l in range(1, LEVELS):
                        h = 1 << l
                        eng.drain()
                        ins = eng.tensor_tensor(half(XL[:, l, two], h, 0), half(k, h, 0), half(suf, h, 0), ALU.mult)
                        if l < LEVELS - 1:
                            right = tot[:, 1, two, 0:PAD // (2 * h)]
                            eng.tensor_tensor(right, half(suf, h, 1)[:, :, :, 0], half(w, h, 1)[:, :, :, 0], ALU.mult)
                            eng.drain()
                            eng.tensor_tensor(half(suf, h, 0), half(suf, h, 0), right.unsqueeze(3).broadcast_to([P, 2, PAD // (2 * h), h]), ALU.mult)
                    ins.then_inc(s_xk, 1)

                def head_rstd(i):
                    eng.wait_ge(s_var, gi * NB + i + 1)
                    eng.tensor_tensor(var[:, :, 0], var[:, :, 0], g.neg_half[0:T, 0:1].broadcast_to([T, HEADS_R]), ALU.pow).then_inc(s_gr, 1)

                def finish(i):
                    b = gi * NB + i
                    inv_std(eng, g, stats[:, i % 2, 7:8], s_xvar, b).then_inc(s_rstd, 1)
                    eng.wait_ge(s_new, b + 1)
                    eng.tensor_copy(X[:, bass.ds(b, 1), :].rearrange("p a n -> p (a n)"), y[:, i % 2, :]).then_inc(s_xsaved, 1)

                left_levels(0, 0)
                left_levels(0, 1)
                for i in range(NB):
                    b = gi * NB + i
                    if i > 0:
                        eng.wait_ge(s_gp, b * 8)
                        left_levels(i, 1)
                        head_rstd(i - 1)
                    if i < NB - 1:
                        eng.wait_ge(s_gp, b * 8 + 4)
                        left_levels(i + 1, 0)
                    if i > 0:
                        finish(i - 1)
                head_rstd(NB - 1)
                finish(NB - 1)
                eng.drain()


HEADS_M, HEAD_M = 16, 32
CLIP = 50.0


def stage_masked_attention(g):
    nc, PS, X, XT = g.nc, g.PS, g.X, g.XT
    with ExitStack() as st:
        sb, sem = g.in_stage(st, "ma_")
        wq, wk, wv, wo = (sb(n, [P, C, D]) for n in ("wq", "wk", "wv", "wo"))
        bias_cols = sb("bias_cols", [P, 2, C])
        bv, bo, gamma, beta = sb("bv", [P, D]), sb("bo", [T, D]), sb("gamma", [T, D]), sb("beta", [T, D])
        rs = sb("rs", [T, 1])
        mask_in = sb("mask_in", [P, B * 3], I32)
        scale, shift = sb("scale", [P, B * 3]), sb("shift", [P, B * 3])
        scale_b, shift_b = sb("scale_b", [P, 3]), sb("shift_b", [P, 3])
        QT = sb("QT", [P, C, B * T])
        qb = sb("qb", [P, C, T])
        ctx = sb("ctx", [P, 2, C, S2])
        KT = sb("KT", [P, 2, C, S2])
        V = sb("V", [P, 2, 3, HEADS_M, HEAD_M + 1])
        E = sb("E", [P, 3, 4, C * T])
        rsum = sb("rsum", [T, HEADS_M])
        o, oT = sb("o", [T, D]), sb("oT", [P, C, T])
        y = sb("y", [T, 2, D])
        stats = sb("stats", [T, 2, 8])
        s_wq = sem("wq_in")
        s_w, s_ones, s_q, s_qt = sem("weights_in"), sem("constants_set"), sem("q_psum"), sem("QT_ready")
        s_ctx = [sem("ctx_even"), sem("ctx_odd")]
        s_k, s_kt, s_v, s_vc, s_qb = sem("k_psum"), sem("KT_ready"), sem("v_psum"), sem("v_taken"), sem("q_and_mask_staged")
        s_s, s_e, s_clip, s_pv, s_o, s_oT, s_oTc, s_wo = (sem(n) for n in ("scores_psum", "exp", "clipped", "pv_psum", "o_ready", "oT_psum", "oT_copied", "wo_psum"))
        s_taken = sem("wo_taken")
        s_var1, s_rstd1, s_var, s_rstd, s_new, s_xsaved = (sem(n) for n in ("delta_var", "delta_rstd", "var", "rstd", "x_new", "x_saved"))
        block = st.enter_context(nc.Block())

        def ctx_rows(b):
            return g.d["ctxT"][bass.ds(b * P, P), :].rearrange("p (c n) -> p c n", c=C)

        @block.sync
        def _(eng):
            eng.dma_start(bias_cols[:, :, :], g.d["ma_bias_cols"].rearrange("p (a c) -> p a c", a=2)).then_inc(s_wq, 16)
            eng.dma_start(wq[:, :, :], g.d["L1_xattn_Wq"].rearrange("p (c n) -> p c n", c=C)).then_inc(s_wq, 16)
            for dst, src in ((wk, "L1_xattn_Wk"), (wv, "L1_xattn_Wv"), (wo, "L1_xattn_Wo")):
                eng.dma_start(dst[:, :, :], g.d[src].rearrange("p (c n) -> p c n", c=C)).then_inc(s_w, 16)
            for dst, src in ((bv, "L1_xattn_bv"), (bo, "L1_xattn_bo"), (gamma, "L1_xattn_ln_gamma"), (beta, "L1_xattn_ln_beta"),
                             (rs, "L1_xattn_residual_scale"), (mask_in, "mask_cols")):
                eng.dma_start(dst[:, :], g.d[src]).then_inc(s_w, 16)
            for par in range(2):
                eng.dma_start(ctx[:, par, :, :], ctx_rows(par)).then_inc(s_ctx[par], 16)
            with eng.Fori(0, PAIRS - 1) as it:
                for par in range(2):
                    eng.wait_ge(s_s, 6 * (it * 2 + par + 1))
                    eng.dma_start(ctx[:, par, :, :], ctx_rows(it * 2 + par + 2)).then_inc(s_ctx[par], 16)

        @block.tensor
        def _(eng):
            eng.wait_ge(s_wq, 16 * 2)
            with eng.Fori(0, B * T // GROUP) as it:
                for c_out in range(C):
                    eng.wait_ge(s_qt, it * C + c_out + 1)
                    for c in range(C):
                        mm = eng.matmul(PS[:, c_out, 0:GROUP], wq[:, c, c_out * P:(c_out + 1) * P], XT[:, c, bass.ds(it * GROUP, GROUP)],
                                        start=c == 0, stop=c == C - 1)
                    mm.then_inc(s_q, 1)
            eng.wait_ge(s_qt, 4 + 16)
            eng.wait_ge(s_w, 16 * 9)
            eng.wait_ge(s_ones, 4)

            def make(it, par, first):
                b = it * 2 + par
                eng.wait_ge(s_ctx[par], 16 * (it + 1))
                if not first:
                    eng.wait_ge(s_taken, b - 1)
                for c_out in range(C):
                    if c_out >= 2:
                        eng.wait_ge(s_kt, b * C + c_out - 1)
                    for c in range(C):
                        mm = eng.matmul(PS[:, c_out % 2, 0:S2], wk[:, c, c_out * P:(c_out + 1) * P], ctx[:, par, c, :], start=c == 0, stop=c == C - 1)
                    mm.then_inc(s_k, 1)
                if par == 1:
                    eng.wait_ge(s_e, b * 6)
                for m, (at, n) in enumerate(CTX):
                    for c in range(C):
                        mm = eng.matmul(PS[0:n, 4 + m, :], ctx[:, par, c, at:at + n], wv[:, c, :], start=c == 0, stop=c == C - 1)
                    mm.then_inc(s_v, 1)
                eng.wait_ge(s_kt, b * C + C)

            def score(it, par):
                b = it * 2 + par
                eng.wait_ge(s_qb, b + 1)
                eng.wait_ge(s_vc, b * 3 + 3)
                for m, (at, n) in enumerate(CTX):
                    for r in range(4):
                        u = 2 * m + r // 2
                        if u >= 2 and r % 2 == 0:
                            eng.wait_ge(s_e, b * 6 + u - 1)
                        for c in range(C):
                            mm = eng.matmul(PS[0:n, 4 + r, c * T:(c + 1) * T], KT[32 * r:32 * r + 32, par, c, at:at + n], qb[32 * r:32 * r + 32, c, :],
                                            start=True, stop=True)
                        if r % 2 == 1:
                            mm.then_inc(s_s, 1)

            def values(it, par):
                b = it * 2 + par
                eng.wait_ge(s_clip, b * 6 + 6)
                eng.wait_ge(s_o, b + 1)
                for h in range(HEADS_M):
                    at = 33 * (h % 8)
                    for m, (_, n) in enumerate(CTX):
                        mm = eng.matmul(PS[0:T, 2 + h // 8, at:at + 33], E[0:n, m, h % 4, (h // 4) * T:(h // 4 + 1) * T], V[0:n, par, m, h, :],
                                        start=m == 0, stop=m == 2)
                mm.then_inc(s_pv, 1)

            def project(b):
                eng.wait_ge(s_o, b + 2)
                for c in range(C):
                    mm = eng.transpose(PS[:, 0, c * T:(c + 1) * T], o[:, c * P:(c + 1) * P], g.ident[0:T, 0:T])
                mm.then_inc(s_oT, 1)
                eng.wait_ge(s_oTc, b + 1)
                for c in range(C):
                    mm = eng.matmul(PS[0:T, 1, :], oT[:, c, :], wo[:, c, :], start=c == 0, stop=c == C - 1)
                mm.then_inc(s_wo, 1)

            def pair(it, first):
                make(it, 0, first)
                if not first:
                    project(it * 2 - 1)
                score(it, 0)
                make(it, 1, first)
                values(it, 0)
                score(it, 1)
                project(it * 2)
                values(it, 1)
            pair(0, True)
            with eng.Fori(1, PAIRS) as it:
                pair(it, False)
            project(B - 1)

        @block.scalar
        def _(eng):
            eng.wait_ge(s_wq, 16 * 2)
            with eng.Fori(0, B * T // GROUP) as it:
                for c in range(C):
                    eng.wait_ge(s_q, it * C + c + 1)
                    eng.activation(QT[:, c, bass.ds(it * GROUP, GROUP)], PS[:, c, 0:GROUP], ACT.Identity, bias=bias_cols[:, 0, c:c + 1]).then_inc(s_qt, 1)

            def k_copies(it, par):
                b = it * 2 + par
                for c in range(C):
                    eng.wait_ge(s_k, b * C + c + 1)
                    eng.activation(KT[:, par, c, :], PS[:, c % 2, 0:S2], ACT.Identity, bias=bias_cols[:, 1, c:c + 1]).then_inc(s_kt, 1)

            def exps(it, par):
                b = it * 2 + par
                eng.wait_ge(s_qb, b + 1)
                if par == 1:
                    eng.wait_ge(s_pv, b)
                for m, (at, n) in enumerate(CTX):
                    for half in range(2):
                        eng.wait_ge(s_s, b * 6 + 2 * m + half + 1)
                        eng.activation(E[0:n, m, 2 * half:2 * half + 2, :], PS[0:n, 4 + 2 * half:6 + 2 * half, 0:C * T], ACT.Exp,
                                       scale=scale_b[0:n, m:m + 1], bias=shift_b[0:n, m:m + 1]).then_inc(s_e, 1)

            def o_copy(b):
                eng.wait_ge(s_oT, b + 1)
                eng.activation(oT[:, :, :], PS[:, 0, 0:C * T].rearrange("p (c t) -> p c t", c=C), ACT.Copy).then_inc(s_oTc, 1)

            def pair(it, first):
                k_copies(it, 0)
                if not first:
                    o_copy(it * 2 - 1)
                    eng.wait_ge(s_pv, it * 2)
                exps(it, 0)
                k_copies(it, 1)
                exps(it, 1)
                o_copy(it * 2)
            pair(0, True)
            with eng.Fori(1, PAIRS) as it:
                pair(it, False)
            o_copy(B - 1)

        @block.vector
        def _(eng):
            eng.sem_inc(s_qt, 4)
            eng.sem_inc(s_o, 1)
            eng.memset(V[:, :, :, :, HEAD_M:HEAD_M + 1], 1.0).then_inc(s_ones, 1)
            eng.wait_ge(s_w, 16 * 9)
            eng.tensor_copy(scale[:, :], mask_in[:, :])
            eng.tensor_scalar(rs[:, :], rs[:, :], 0.0, 0.3, ALU.max, ALU.min).then_inc(s_ones, 1)
            eng.drain()
            eng.tensor_scalar(scale[:, :], scale[:, :], 0.5, None, ALU.is_gt)
            eng.drain()
            eng.tensor_scalar(shift[:, :], scale[:, :], CLIP, -CLIP, ALU.mult, ALU.add).then_inc(s_ones, 1)
            eng.drain()
            eng.tensor_scalar(scale[:, :], scale[:, :], HEAD_M ** -0.5, None, ALU.mult).then_inc(s_ones, 1)
            eng.wait_ge(s_qt, 4 + 16)
            eng.drain()

            def stage(it, par):
                b = it * 2 + par
                eng.tensor_copy(qb[:, :, :], QT[:, :, bass.ds(b * T, T)])
                eng.tensor_copy(scale_b[:, :], scale[:, bass.ds(b * 3, 3)])
                eng.tensor_copy(shift_b[:, :], shift[:, bass.ds(b * 3, 3)])
                eng.drain().then_inc(s_qb, 1)
                for m, (at, n) in enumerate(CTX):
                    eng.wait_ge(s_v, b * 3 + m + 1)
                    eng.tensor_tensor(V[0:n, par, m, :, 0:HEAD_M], PS[0:n, 4 + m, :].rearrange("p (h d) -> p h d", d=HEAD_M),
                                      bv[0:n, :].rearrange("p (h d) -> p h d", d=HEAD_M), ALU.add).then_inc(s_vc, 1)

            def clip(it, par):
                b = it * 2 + par
                for m, (at, n) in enumerate(CTX):
                    for half in range(2):
                        eng.wait_ge(s_e, b * 6 + 2 * m + half + 1)
                        e = E[0:n, m, 2 * half:2 * half + 2, :]
                        eng.tensor_scalar(e, e, float(np.exp(-CLIP)), float(np.exp(CLIP)), ALU.max, ALU.min).then_inc(s_clip, 1)

            def normalise(b):
                eng.wait_ge(s_pv, b + 1)
                o4 = PS[0:T, 2:4, 0:264].rearrange("p a (h d) -> p a h d", d=33)
                r3 = rsum[:, :].rearrange("p (a h) -> p a h", a=2)
                eng.tensor_scalar(r3, o4[:, :, :, HEAD_M], 1.0 + 1e-8, None, ALU.mult)
                eng.drain()
                eng.reciprocal(rsum[:, :], rsum[:, :])
                eng.drain()
                for a in range(2):
                    ins = eng.tensor_tensor(o[:, 256 * a:256 * a + 256].rearrange("p (h d) -> p h d", d=HEAD_M), o4[:, a, :, 0:HEAD_M],
                                            r3[:, a, :].unsqueeze(2).broadcast_to([T, 8, HEAD_M]), ALU.mult)
                ins.then_inc(s_o, 1)

            def finish(b, par):
                yb = y[:, par, :]
                eng.wait_ge(s_wo, b + 1)
                eng.wait_ge(s_xsaved, b + 1)
                eng.tensor_tensor(yb, PS[0:T, 1, :], bo[:, :], ALU.add).then_inc(s_taken, 1)
                eng.drain()
                eng.tensor_scalar(yb, yb, rs[:, 0:1], None, ALU.mult)
                layer_norm(eng, yb, stats[:, par, :], s_var1, s_rstd1, b)
                eng.drain()
                eng.tensor_tensor(yb, yb, gamma[:, :], ALU.mult)
                eng.drain()
                eng.tensor_tensor(yb, yb, beta[:, :], ALU.add)
                eng.drain()
                eng.tensor_tensor(yb, yb, X[:, bass.ds(b, 1), :].rearrange("p a n -> p (a n)"), ALU.add)
                layer_norm(eng, yb, stats[:, par, :], s_var, s_rstd, b).then_inc(s_new, 1)

            def pair(it, first):
                stage(it, 0)
                if not first:
                    finish(it * 2 - 1, 1)
                clip(it, 0)
                stage(it, 1)
                normalise(it * 2)
                clip(it, 1)
                finish(it * 2, 0)
                normalise(it * 2 + 1)
            pair(0, True)
            with eng.Fori(1, PAIRS) as it:
                pair(it, False)
            finish(B - 1, 1)

        @block.gpsimd
        def _(eng):
            eng.sem_inc(s_xsaved, 2)
            with eng.Fori(0, PAIRS) as it:
                for par in range(2):
                    b = it * 2 + par
                    inv_std(eng, g, stats[:, par, 7:8], s_var1, b).then_inc(s_rstd1, 1)
                    inv_std(eng, g, stats[:, par, 7:8], s_var, b).then_inc(s_rstd, 1)
                    eng.wait_ge(s_new, b + 1)
                    eng.tensor_copy(X[:, bass.ds(b, 1), :].rearrange("p a n -> p (a n)"), y[:, par, :]).then_inc(s_xsaved, 1)


TAKEN = T // 8
SEL = B * TAKEN
HALF = SEL // 2
HEAD_D = 128
Q_HEADS, KV_HEADS = 16, 8
INNER = 2048
FAR = -3.0e38


def stage_routed_block(g):
    nc, PS, X = g.nc, g.PS, g.X
    with ExitStack() as st:
        sb, sem = g.in_stage(st, "rb_")
        w_a, w_b, w_c = (sb(n, [P, 4 * INNER]) for n in ("w_a", "w_b", "w_c"))
        wide = [w[:, :].rearrange("p (c n) -> p c n", c=C) for w in (w_a, w_b)]
        wk, wv = (w_b[:, n * C * 1024:(n + 1) * C * 1024].rearrange("p (c n) -> p c n", c=C) for n in range(2))
        tall = w_c[:, :].rearrange("p (k n) -> p k n", k=16)
        out_mem = sb("out_mem", [T, 2 * D])
        router = out_mem[:, 0:D]
        block_out = out_mem[0:HALF, :].rearrange("p (t n) -> p t n", t=2)
        tri, ones = sb("tri", [T, T]), sb("ones", [P, P])
        below = sb("below", [T, T])
        slots = sb("slots", [T, TAKEN])
        cos_t, sin_t = sb("cos_t", [T, HEAD_D]), sb("sin_t", [T, HEAD_D])
        rotate = sb("rotate", [P, P])
        causal = sb("causal", [HALF, 3 * HALF])
        cols = sb("cols", [P, Q_HEADS + KV_HEADS + C])
        bv, ln2 = sb("bv", [HALF, 1024]), sb("ln2", [HALF, D])
        eps = sb("eps", [P, 1])
        XTf = g.XT[:, :, :].rearrange("p c n -> p (c n)")
        diag, eq, gt = (XTf[0:T, n * B * T:(n + 1) * B * T].rearrange("p (b s) -> p b s", b=B) for n in range(3))
        prod = XTf[0:T, 3 * B * T:3 * B * T + 2 * D].rearrange("p (b n) -> p b n", b=2)
        score, own, rank, sel, gate, keep = (sb(n, [T, B]) for n in ("score", "own", "rank", "sel", "gate", "keep"))
        pick = sb("pick", [T, B, TAKEN])
        v_mem = sb("v_mem", [T, 2048])
        pick_f = v_mem[:, 0:2 * 8 * 108].rearrange("p (g n) -> p g n", g=2)
        v = v_mem[0:HALF, :].rearrange("p (t n) -> p t n", t=2)
        y = v_mem[:, 0:2 * D].rearrange("p (t n) -> p t n", t=2)
        xT = sb("xT", [P, C, SEL])
        hT = xT
        xr = sb("xr", [HALF, 2, D])
        cosT, sinT = sb("cosT", [P, SEL]), sb("sinT", [P, SEL])
        rinv = sb("rinv", [P, SEL])
        qk = XTf[:, 0:(Q_HEADS + KV_HEADS) * SEL].rearrange("p (h s) -> p h s", s=SEL)
        pick_T = XTf[0:HALF, (Q_HEADS + KV_HEADS) * SEL:(Q_HEADS + KV_HEADS) * SEL + B * T].rearrange("p (b t) -> p b t", t=T)
        turned = sb("turned", [P, 2, 2 * SEL])
        sq = turned[:, :, :].rearrange("p a (c s) -> p (a c) s", s=SEL)
        att_mem = sb("att_mem", [P, 4 * 3 * HALF])
        S, PT = (att_mem[0:HALF, n * 6 * HALF:(n + 1) * 6 * HALF].rearrange("p (a n) -> p a n", a=2) for n in range(2))
        th = att_mem[:, 0:4 * SEL].rearrange("p (a n) -> p a n", a=2)
        top, total = sb("top", [HALF, 2, 2]), sb("total", [HALF, 2, 2])
        aoT = sb("aoT", [P, Q_HEADS, SEL])
        ms = sb("ms", [HALF, 2])
        stats = sb("stats", [T, 2, 8])
        s_c, s_set = sem("constants_in"), sem("eps_set")
        s_wa, s_wb, s_wc = sem("wq_gate_in"), sem("wkv_up_in"), sem("wo_down_in")
        s_score, s_gexp = sem("scores_ready"), sem("gate_exp")
        s_diag, s_row, s_sel, s_slot, s_pick = sem("diag"), sem("row_psum"), sem("selected"), sem("slot_psum"), sem("pick")
        s_pT, s_pTc, s_x, s_xc, s_xr, s_xrc, s_cs, s_csc = (sem(n) for n in ("pickT_psum", "pickT_copied", "xT_psum", "xT_copied", "xr_psum", "xr_copied", "cos_psum", "cos_copied"))
        s_sq, s_ms, s_ri, s_h = sem("squares"), sem("meansq_psum"), sem("rinv"), sem("hT")
        s_qk, s_qkc, s_rot, s_rope, s_v, s_vc = (sem(n) for n in ("qk_psum", "qk_copied", "rotated_psum", "rope", "v_psum", "v_taken"))
        s_s, s_m, s_e, s_p, s_t, s_tc, s_ao, s_aoc = (sem(n) for n in ("att_psum", "att_max", "att_exp", "att_prob", "probT_psum", "probT_copied", "ao_psum", "ao_copied"))
        s_wo, s_x1, s_ms2, s_r2, s_h2, s_h2T, s_h2Tc = (sem(n) for n in ("wo_psum", "x1", "x1_squares", "x1_rinv", "h2", "h2T_psum", "h2T_copied"))
        s_gu, s_th, s_hid, s_dn, s_out = sem("gate_up_psum"), sem("tanh"), sem("hidden"), sem("down_psum"), sem("block_out")
        s_sc, s_var, s_rstd, s_new = sem("scattered_psum"), sem("var"), sem("rstd"), sem("x_new")
        s_wr = [sem("written_even"), sem("written_odd")]
        block = st.enter_context(nc.Block())
        SQ_HALF = [slice(0, HALF), slice(HALF, SEL)]

        @block.sync
        def _(eng):
            eng.dma_start(router, g.d["L1_ffn_w_router"]).then_inc(s_c, 16)
            for dst, src in ((tri, "tri"), (below, "below"), (slots, "slots"), (cos_t, "cos_t"), (sin_t, "sin_t"),
                             (rotate, "rotate"), (causal, "causal"), (cols, "rb_cols"), (bv, "L1_ffn_bv"), (ln2, "L1_ffn_ln2_w")):
                eng.dma_start(dst[:, :], g.d[src]).then_inc(s_c, 16)
            eng.dma_start(w_a[:, :], g.d["L1_ffn_wq"]).then_inc(s_wa, 16)
            eng.dma_start(w_b[:, 0:C * 1024], g.d["L1_ffn_wk"]).then_inc(s_wb, 16)
            eng.dma_start(w_b[:, C * 1024:], g.d["L1_ffn_wv"]).then_inc(s_wb, 16)
            eng.dma_start(w_c[:, :], g.d["L1_ffn_wo"]).then_inc(s_wc, 16)
            eng.wait_ge(s_qk, 12)
            eng.dma_start(w_a[:, :], g.d["L1_ffn_w_gate"]).then_inc(s_wa, 16)
            eng.wait_ge(s_v, 4)
            eng.dma_start(w_b[:, :], g.d["L1_ffn_w_up"]).then_inc(s_wb, 16)
            eng.wait_ge(s_wo, 2)
            eng.dma_start(w_c[:, :], g.d["L1_ffn_w_down"]).then_inc(s_wc, 16)
            for b in range(B):
                eng.wait_ge(s_new, b + 1)
                eng.dma_start(g.out[b, :, :], y[:, b % 2, :]).then_inc(s_wr[b % 2], 16)
            for par in range(2):
                eng.wait_ge(s_wr[par], 16 * PAIRS)

        def rotate_unit(eng, u):
            eng.wait_ge(s_qkc, u + 1)
            if u >= 2:
                eng.wait_ge(s_rope, u - 1)
            eng.matmul(PS[:, 6 + u % 2, 0:2 * SEL], rotate[:, :], qk[:, 2 * u:2 * u + 2, :].rearrange("p h s -> p (h s)"), start=True, stop=True).then_inc(s_rot, 1)

        @block.tensor
        def _(eng):
            eng.wait_ge(s_c, 16 * 11)
            eng.wait_ge(s_set, 2)
            eng.wait_ge(s_diag, 1)
            dflat = diag.rearrange("p b s -> p (b s)")
            for n in range(4):
                mm = eng.matmul(PS[0:T, n, 0:GROUP], ones[0:T, 0:T], dflat[:, n * GROUP:(n + 1) * GROUP], start=True, stop=True)
            mm.then_inc(s_row, 1)
            eng.wait_ge(s_sel, 1)
            eng.matmul(PS[0:T, 4, 0:B], tri[:, :], sel[:, :], start=True, stop=True).then_inc(s_slot, 1)
            eng.wait_ge(s_pick, 1)
            for c in range(C):
                for b in range(B):
                    at = (c % 2) * SEL + b * TAKEN
                    mm = eng.matmul(PS[:, c // 2, at:at + TAKEN], X[:, b, c * P:(c + 1) * P], pick[:, b, :], start=True, stop=True)
            mm.then_inc(s_x, 1)
            for n, table in enumerate((cos_t, sin_t)):
                mm = eng.matmul(PS[:, 2, n * SEL:(n + 1) * SEL], table[:, :], pick[:, :, :].rearrange("p b j -> p (b j)"), start=True, stop=True)
            mm.then_inc(s_cs, 1)
            for b in range(B):
                mm = eng.transpose(PS[0:HALF, 4 + b // 4, (b % 4) * T:(b % 4 + 1) * T], pick_f[:, b // 8, (b % 8) * HALF:(b % 8 + 1) * HALF], g.ident[0:T, 0:T])
            mm.then_inc(s_pT, 1)
            eng.wait_ge(s_xc, 1)
            eng.wait_ge(s_csc, 1)
            for t in range(2):
                for c in range(C):
                    mm = eng.transpose(PS[0:HALF, t, c * P:(c + 1) * P], xT[:, c, SQ_HALF[t]], g.ident[:, :])
            mm.then_inc(s_xr, 1)
            eng.wait_ge(s_sq, 1)
            for c in range(C):
                mm = eng.matmul(PS[:, 2, 0:SEL], ones[:, :], sq[:, c, :], start=c == 0, stop=c == C - 1)
            mm.then_inc(s_ms, 1)
            eng.wait_ge(s_h, 1)
            eng.wait_ge(s_pTc, 1)
            for u in range(12):
                if u == 0:
                    eng.wait_ge(s_wa, 16)
                if u == 8:
                    eng.wait_ge(s_wb, 32)
                if u >= 2:
                    eng.wait_ge(s_qkc, u - 1)
                for j in range(2):
                    h = 2 * u + j
                    w, at = (wide[0], h * P) if h < Q_HEADS else (wk, (h - Q_HEADS) * P)
                    for c in range(C):
                        mm = eng.matmul(PS[:, 4 + u % 2, j * SEL:(j + 1) * SEL], w[:, c, at:at + P], hT[:, c, :], start=c == 0, stop=c == C - 1)
                mm.then_inc(s_qk, 1)
                if u >= 1:
                    rotate_unit(eng, u - 1)
            rotate_unit(eng, 11)
            eng.wait_ge(s_xrc, 1)
            for n in range(4):
                t, part = n // 2, n % 2
                for c in range(C):
                    mm = eng.matmul(PS[0:HALF, n, :], hT[:, c, SQ_HALF[t]], wv[:, c, part * 512:(part + 1) * 512], start=c == 0, stop=c == C - 1)
                mm.then_inc(s_v, 1)
            eng.wait_ge(s_rope, 12)
            eng.wait_ge(s_vc, 4)

            def scores(h):
                if h >= 2:
                    eng.wait_ge(s_m, h - 1)
                k = Q_HEADS + h // 2
                eng.matmul(PS[0:HALF, h % 2, 0:HALF], qk[:, h, 0:HALF], qk[:, k, 0:HALF], start=True, stop=True)
                eng.matmul(PS[0:HALF, h % 2, HALF:3 * HALF], qk[:, h, HALF:SEL], qk[:, k, :], start=True, stop=True).then_inc(s_s, 1)

            def turn(h):
                eng.wait_ge(s_p, h + 1)
                if h >= 2:
                    eng.wait_ge(s_tc, h - 1)
                for n in range(3):
                    mm = eng.transpose(PS[0:HALF, 2 + h % 2, n * HALF:(n + 1) * HALF], S[:, h % 2, n * HALF:(n + 1) * HALF], g.ident[0:HALF, 0:HALF])
                mm.then_inc(s_t, 1)

            def values(h):
                eng.wait_ge(s_tc, h + 1)
                if h >= 2:
                    eng.wait_ge(s_aoc, h - 1)
                at = (h // 2) * HEAD_D
                eng.matmul(PS[:, 4 + h % 2, 0:HALF], v[:, 0, at:at + HEAD_D], PT[:, h % 2, 0:HALF], start=True, stop=True)
                eng.matmul(PS[:, 4 + h % 2, HALF:SEL], v[:, 0, at:at + HEAD_D], PT[:, h % 2, HALF:2 * HALF], start=True, stop=False)
                eng.matmul(PS[:, 4 + h % 2, HALF:SEL], v[:, 1, at:at + HEAD_D], PT[:, h % 2, 2 * HALF:3 * HALF], start=False, stop=True).then_inc(s_ao, 1)
            for h in range(Q_HEADS + 2):
                if h < Q_HEADS:
                    scores(h)
                if 1 <= h <= Q_HEADS:
                    turn(h - 1)
                if h >= 2:
                    values(h - 2)
            eng.wait_ge(s_aoc, Q_HEADS)
            eng.wait_ge(s_wc, 16)
            for t in range(2):
                for h in range(Q_HEADS):
                    mm = eng.matmul(PS[0:HALF, 6 + t, :], aoT[:, h, SQ_HALF[t]], tall[:, h, :], start=h == 0, stop=h == Q_HEADS - 1)
                mm.then_inc(s_wo, 1)
            eng.wait_ge(s_h2, 1)
            for c in range(C):
                for t in range(2):
                    mm = eng.transpose(PS[:, c // 2, (c % 2) * SEL + t * HALF:(c % 2) * SEL + (t + 1) * HALF], block_out[:, t, c * P:(c + 1) * P], g.ident[0:HALF, 0:HALF])
            mm.then_inc(s_h2T, 1)
            eng.wait_ge(s_h2Tc, 1)
            eng.wait_ge(s_wa, 32)
            eng.wait_ge(s_wb, 48)
            for u in range(8):
                if u >= 2:
                    eng.wait_ge(s_hid, u - 1)
                for n in range(2):
                    for j in range(2):
                        at = (2 * u + j) * P
                        for c in range(C):
                            mm = eng.matmul(PS[:, 2 * n + u % 2, j * SEL:(j + 1) * SEL], wide[n][:, c, at:at + P], hT[:, c, :], start=c == 0, stop=c == C - 1)
                mm.then_inc(s_gu, 1)
            eng.wait_ge(s_hid, 8)
            eng.wait_ge(s_wc, 32)
            for t in range(2):
                for k in range(16):
                    mm = eng.matmul(PS[0:HALF, 4 + t, :], aoT[:, k, SQ_HALF[t]], tall[:, k, :], start=k == 0, stop=k == 15)
                mm.then_inc(s_dn, 1)
            eng.wait_ge(s_out, 1)
            for b in range(B):
                if b >= 4:
                    eng.wait_ge(s_new, b - 3)
                eng.matmul(PS[0:T, b % 4, :], pick_T[:, b, :], block_out[:, b // 8, :], start=True, stop=True).then_inc(s_sc, 1)

        @block.scalar
        def _(eng):
            eng.wait_ge(s_c, 16 * 11)
            eng.wait_ge(s_set, 2)
            eng.wait_ge(s_score, 1)
            eng.activation(gate[:, :], score[:, :], ACT.Exp, scale=-1.0).then_inc(s_gexp, 1)
            eng.wait_ge(s_x, 1)
            eng.activation(xT[:, :, :].rearrange("p (a c) s -> p a (c s)", a=2), PS[:, 0:2, 0:2 * SEL], ACT.Copy).then_inc(s_xc, 1)
            eng.activation(turned[:, :, :], PS[:, 0:2, 0:2 * SEL], ACT.Square).then_inc(s_sq, 1)
            eng.wait_ge(s_cs, 1)
            eng.activation(cosT[:, :], PS[:, 2, 0:SEL], ACT.Copy)
            eng.activation(sinT[:, :], PS[:, 2, SEL:2 * SEL], ACT.Copy).then_inc(s_csc, 1)
            eng.wait_ge(s_pT, 1)
            eng.activation(pick_T[:, :, :].rearrange("p (a b) t -> p a (b t)", a=4), PS[0:HALF, 4:8, 0:GROUP], ACT.Copy).then_inc(s_pTc, 1)
            eng.wait_ge(s_xr, 1)
            eng.activation(xr[:, :, :], PS[0:HALF, 0:2, :], ACT.Copy).then_inc(s_xrc, 1)
            eng.wait_ge(s_ms, 1)
            eng.activation(rinv[:, :], PS[:, 2, 0:SEL], ACT.Ln, scale=1.0 / D, bias=eps[:, 0:1])
            eng.drain()
            eng.activation(rinv[:, :], rinv[:, :], ACT.Exp, scale=-0.5).then_inc(s_ri, 1)
            for u in range(12):
                eng.wait_ge(s_qk, u + 1)
                for j in range(2):
                    ins = eng.activation(qk[:, 2 * u + j, :], PS[:, 4 + u % 2, j * SEL:(j + 1) * SEL], ACT.Identity, bias=cols[:, 2 * u + j:2 * u + j + 1])
                ins.then_inc(s_qkc, 1)
            for h in range(Q_HEADS + 2):
                if h < Q_HEADS:
                    eng.wait_ge(s_m, h + 1)
                    for t, part in enumerate((slice(0, HALF), slice(HALF, 3 * HALF))):
                        ins = eng.activation(S[:, h % 2, part], S[:, h % 2, part], ACT.Exp, bias=top[:, h % 2, t:t + 1], accum_out=total[:, h % 2, t:t + 1])
                    ins.then_inc(s_e, 1)
                if 1 <= h <= Q_HEADS:
                    eng.wait_ge(s_t, h)
                    eng.activation(PT[:, (h - 1) % 2, :], PS[0:HALF, 2 + (h - 1) % 2, 0:3 * HALF], ACT.Copy).then_inc(s_tc, 1)
                if h >= 2:
                    eng.wait_ge(s_ao, h - 1)
                    eng.activation(aoT[:, h - 2, :], PS[:, 4 + h % 2, 0:SEL], ACT.Copy).then_inc(s_aoc, 1)
            for t in range(2):
                eng.wait_ge(s_x1, t + 1)
                ins = eng.activation(block_out[:, t, :], xr[:, t, :], ACT.Square, accum_out=ms[:, t:t + 1])
            eng.drain()
            eng.activation(ms[:, :], ms[:, :], ACT.Ln, scale=1.0 / D, bias=eps[0:HALF, 0:1])
            eng.drain()
            eng.activation(ms[:, :], ms[:, :], ACT.Exp, scale=-0.5).then_inc(s_r2, 1)
            eng.wait_ge(s_h2T, 1)
            eng.activation(hT[:, :, :].rearrange("p (a c) s -> p a (c s)", a=2), PS[:, 0:2, 0:2 * SEL], ACT.Copy).then_inc(s_h2Tc, 1)
            for u in range(8):
                eng.wait_ge(s_gu, u + 1)
                eng.activation(th[:, u % 2, :], PS[:, u % 2, 0:2 * SEL], ACT.Tanh, scale=0.5).then_inc(s_th, 1)

        @block.vector
        def _(eng):
            eng.memset(ones[:, :], 1.0).then_inc(s_set, 1)
            eng.memset(eps[:, :], 1e-6).then_inc(s_set, 1)
            eng.memset(v_mem[:, :], 0.0)
            eng.wait_ge(s_c, 16 * 11)
            per_pair = [T, B, T]
            for n in range(PAIRS):
                eng.drain()
                eng.tensor_tensor(prod, X[:, 2 * n:2 * n + 2, :], router.unsqueeze(1).broadcast_to([T, 2, D]), ALU.mult)
                eng.drain()
                eng.tensor_reduce(score[:, 2 * n:2 * n + 2], prod, AX.X, ALU.add)
            eng.drain().then_inc(s_score, 1)
            ident = g.ident[0:T, 0:T].unsqueeze(1).broadcast_to(per_pair)
            eng.tensor_tensor(diag, ident, score[:, :].unsqueeze(2).broadcast_to(per_pair), ALU.mult).then_inc(s_diag, 1)
            eng.wait_ge(s_row, 1)
            rows = PS[0:T, 0:4, 0:GROUP].rearrange("p a (b s) -> p a b s", s=T)

            def by_bank(a):
                return a.rearrange("p (a b) s -> p a b s", a=4)
            for n in range(4):
                part = slice(4 * n, 4 * n + 4)
                eng.tensor_tensor(eq[:, part, :], rows[:, n], g.ident[0:T, 0:T].unsqueeze(1).broadcast_to([T, 4, T]), ALU.mult)
            eng.drain()
            eng.tensor_reduce(own[:, :], eq, AX.X, ALU.add)
            eng.drain()
            for n in range(4):
                part = slice(4 * n, 4 * n + 4)
                mine = own[:, part].unsqueeze(2).broadcast_to([T, 4, T])
                eng.tensor_tensor(gt[:, part, :], rows[:, n], mine, ALU.is_gt)
                eng.tensor_tensor(eq[:, part, :], rows[:, n], mine, ALU.is_equal)
            eng.drain()
            eng.tensor_tensor(eq, eq, below[:, :].unsqueeze(1).broadcast_to(per_pair), ALU.mult)
            eng.drain()
            eng.tensor_tensor(gt, gt, eq, ALU.add)
            eng.drain()
            eng.tensor_reduce(rank[:, :], gt, AX.X, ALU.add)
            eng.drain()
            eng.tensor_scalar(sel[:, :], rank[:, :], TAKEN - 0.5, None, ALU.is_lt).then_inc(s_sel, 1)
            eng.wait_ge(s_gexp, 1)
            eng.tensor_scalar(gate[:, :], gate[:, :], 1.0, None, ALU.add)
            eng.drain()
            eng.reciprocal(gate[:, :], gate[:, :])
            eng.drain()
            eng.tensor_tensor(keep[:, :], gate[:, :], sel[:, :], ALU.mult)
            eng.drain()
            eng.tensor_scalar(keep[:, :], keep[:, :], -1.0, 2.0, ALU.mult, ALU.add)
            eng.wait_ge(s_slot, 1)
            slot_shape = [T, B, TAKEN]
            eng.tensor_tensor(pick[:, :, :], slots[:, :].unsqueeze(1).broadcast_to(slot_shape), PS[0:T, 4, 0:B].unsqueeze(2).broadcast_to(slot_shape), ALU.is_equal)
            eng.drain()
            eng.tensor_tensor(pick[:, :, :], pick[:, :, :], sel[:, :].unsqueeze(2).broadcast_to(slot_shape), ALU.mult)
            eng.drain()
            eng.tensor_copy(pick_f[:, :, :].rearrange("p g (b q) -> p g b q", q=108)[:, :, :, 0:TAKEN], pick[:, :, :].rearrange("p (g b) j -> p g b j", g=2)).then_inc(s_pick, 1)
            eng.wait_ge(s_ri, 1)
            for c in range(C):
                ins = eng.scalar_tensor_tensor(hT[:, c, :], xT[:, c, :], cols[:, Q_HEADS + KV_HEADS + c:Q_HEADS + KV_HEADS + c + 1], rinv[:, :], ALU.mult, ALU.mult)
            ins.then_inc(s_h, 1)
            two = [P, 2, SEL]
            for u in range(12):
                eng.wait_ge(s_rot, u + 1)
                tu = turned[:, u % 2, :].rearrange("p (h s) -> p h s", h=2)
                eng.tensor_tensor(tu, PS[:, 6 + u % 2, 0:2 * SEL].rearrange("p (h s) -> p h s", h=2), sinT[:, :].unsqueeze(1).broadcast_to(two), ALU.mult)
                q2 = qk[:, 2 * u:2 * u + 2, :]
                eng.tensor_tensor(q2, q2, cosT[:, :].unsqueeze(1).broadcast_to(two), ALU.mult)
                eng.drain()
                eng.tensor_tensor(q2, q2, tu, ALU.add).then_inc(s_rope, 1)
            for n in range(4):
                eng.wait_ge(s_v, n + 1)
                eng.tensor_tensor(v[:, n // 2, (n % 2) * 512:(n % 2 + 1) * 512], PS[0:HALF, n, :], bv[:, (n % 2) * 512:(n % 2 + 1) * 512], ALU.add).then_inc(s_vc, 1)
            for h in range(Q_HEADS + 1):
                if h < Q_HEADS:
                    eng.wait_ge(s_s, h + 1)
                    if h >= 2:
                        eng.wait_ge(s_t, h - 1)
                    eng.scalar_tensor_tensor(S[:, h % 2, :], PS[0:HALF, h % 2, 0:3 * HALF], HEAD_D ** -0.5, causal[:, :], ALU.mult, ALU.add)
                    eng.drain()
                    eng.tensor_reduce(top[:, h % 2, 0:1], S[:, h % 2, 0:HALF], AX.X, ALU.max)
                    eng.tensor_reduce(top[:, h % 2, 1:2], S[:, h % 2, HALF:3 * HALF], AX.X, ALU.max)
                    eng.drain()
                    eng.tensor_scalar(top[:, h % 2, :], top[:, h % 2, :], -1.0, None, ALU.mult).then_inc(s_m, 1)
                if h >= 1:
                    k = h - 1
                    eng.wait_ge(s_e, k + 1)
                    eng.reciprocal(total[:, k % 2, :], total[:, k % 2, :])
                    eng.drain()
                    eng.tensor_scalar(S[:, k % 2, 0:HALF], S[:, k % 2, 0:HALF], total[:, k % 2, 0:1], None, ALU.mult)
                    eng.tensor_scalar(S[:, k % 2, HALF:3 * HALF], S[:, k % 2, HALF:3 * HALF], total[:, k % 2, 1:2], None, ALU.mult).then_inc(s_p, 1)
            eng.wait_ge(s_xrc, 1)
            for t in range(2):
                eng.wait_ge(s_wo, t + 1)
                eng.tensor_tensor(xr[:, t, :], xr[:, t, :], PS[0:HALF, 6 + t, :], ALU.add).then_inc(s_x1, 1)
            eng.wait_ge(s_r2, 1)
            eng.drain()
            for t in range(2):
                ins = eng.scalar_tensor_tensor(block_out[:, t, :], xr[:, t, :], ms[:, t:t + 1], ln2[:, :], ALU.mult, ALU.mult)
            ins.then_inc(s_h2, 1)
            for u in range(8):
                eng.wait_ge(s_th, u + 1)
                tu = turned[:, u % 2, :]
                eng.scalar_tensor_tensor(tu, th[:, u % 2, :], 1.0, PS[:, u % 2, 0:2 * SEL], ALU.add, ALU.mult)
                eng.drain()
                eng.scalar_tensor_tensor(aoT[:, 2 * u:2 * u + 2, :].rearrange("p h s -> p (h s)"), tu, 0.5, PS[:, 2 + u % 2, 0:2 * SEL], ALU.mult, ALU.mult).then_inc(s_hid, 1)
            for t in range(2):
                eng.wait_ge(s_dn, t + 1)
                ins = eng.tensor_tensor(block_out[:, t, :], xr[:, t, :], PS[0:HALF, 4 + t, :], ALU.add)
            ins.then_inc(s_out, 1)
            for b in range(B):
                if b >= 2:
                    eng.wait_ge(s_wr[b % 2], 16 * (b // 2))
                yb = y[:, b % 2, :]
                eng.tensor_scalar(yb, X[:, b, :], keep[:, b:b + 1], None, ALU.mult)
                eng.wait_ge(s_sc, b + 1)
                eng.drain()
                eng.scalar_tensor_tensor(yb, PS[0:T, b % 4, :], gate[:, b:b + 1], yb, ALU.mult, ALU.add)
                layer_norm(eng, yb, stats[:, b % 2, :], s_var, s_rstd, b).then_inc(s_new, 1)

        @block.gpsimd
        def _(eng):
            for b in range(B):
                inv_std(eng, g, stats[:, b % 2, 7:8], s_var, b).then_inc(s_rstd, 1)


class Stage:
    pass


def build(nc, dram, out, stages):
    g = Stage()
    g.nc, g.d, g.out = nc, dram, out
    with ExitStack() as ctx:
        g.PS = ctx.enter_context(nc.psum_tensor("PS", [P, 8, 512], F32))
        g.X = ctx.enter_context(nc.sbuf_tensor("X", [T, B, D], F32))
        g.XT = ctx.enter_context(nc.sbuf_tensor("XT", [P, C, B * T], F32))
        g.ident = ctx.enter_context(nc.sbuf_tensor("ident", [P, P], F32))
        g.neg_half = ctx.enter_context(nc.sbuf_tensor("neg_half", [P, 1], F32))

        g.eps = ctx.enter_context(nc.sbuf_tensor("eps", [P, 1], F32))

        def in_stage(st, prefix):
            def sem(name):
                g.sems.append(nc.alloc_semaphore(name=prefix + name))
                return g.sems[-1]
            return lambda name, shape, dt=F32: st.enter_context(nc.sbuf_tensor(prefix + name, shape, dt)), sem
        g.in_stage = in_stage
        for s in stages:
            g.sems = []
            s(g)
            if s is not stages[-1]:
                nc.clear_and_free_semaphores(g.sems)
                nc.all_engine_barrier()


def rows_on_partitions(a):
    r, n = a.shape
    return np.ascontiguousarray(a.reshape(r // P, P, n).transpose(1, 0, 2).reshape(P, -1))


def pair_mask():
    s, t = np.arange(T)[:, None], np.arange(T)[None, :]
    levels = [(s // (2 * h) == t // (2 * h)) & (s % (2 * h) < h) & (t % (2 * h) >= h) for h in (1 << l for l in range(LEVELS))]
    return np.concatenate(levels + [s == t], 1).astype(np.float32)


def constants():
    k, n = np.arange(1, 16)[:, None], np.arange(32)[None, :]
    cos, sin, alt = np.cos(2 * np.pi * k * n / 32), np.sin(2 * np.pi * k * n / 32), (-1.0) ** n
    fwd = np.concatenate([np.full((1, 32), 32 ** -0.5), cos / 4, alt * 32 ** -0.5, sin / 4])
    inv = np.concatenate([np.full((1, 32), 1 / 32), cos / 32, alt / 32, sin / 32])
    dft = np.kron(np.eye(4), fwd.T)
    idft = np.kron(np.eye(4), inv.T)
    inv_freq = 1.0 / np.float32(10000.0) ** (np.arange(0, HEAD_D, 2, dtype=np.float32) / HEAD_D)
    angles = (np.arange(T, dtype=np.float32)[:, None] * inv_freq).astype(np.float32)
    angles = np.concatenate([angles, angles], 1)
    rotate = np.zeros((P, P), np.float32)
    rotate[np.arange(64) + 64, np.arange(64)] = -1
    rotate[np.arange(64), np.arange(64) + 64] = 1
    hidden = np.where(np.tril(np.ones((HALF, HALF), bool)), 0, FAR)
    causal = np.concatenate([hidden, np.zeros((HALF, HALF)), hidden], 1).astype(np.float32)
    return {"dft": dft.astype(np.float32), "idft": idft.astype(np.float32),
            "ones_head16": np.kron(np.eye(8), np.full((16, 16), 1 / 16)).astype(np.float32),
            "earlier": np.ascontiguousarray(np.broadcast_to(np.tril(np.ones((ROUTED, ROUTED), np.float32), -1).reshape(1, -1), (T, ROUTED * ROUTED))),
            "pair_mask": pair_mask(),
            "below": np.tril(np.ones((T, T), np.float32), -1),
            "slots": np.ascontiguousarray(np.broadcast_to(np.arange(1, TAKEN + 1, dtype=np.float32), (T, TAKEN))),
            "cos_t": np.cos(angles), "sin_t": np.sin(angles), "rotate": rotate, "causal": causal,
            "parity": np.stack([np.arange(P) // 16 % 2 == 0, np.arange(P) // 16 % 2 == 1], 1).astype(np.float32),
            "tri": np.triu(np.ones((T, T), np.float32)), "ident": np.eye(P, dtype=np.float32)}


STAGES = [stage_fft_attention, stage_context_attention, stage_experts, stage_recurrence, stage_masked_attention, stage_routed_block]


def kernel(**inputs):
    import concourse.bacc as _bacc
    from concourse.bass_utils import run_bass_kernel_spmd as _run
    i = {k: np.asarray(v) for k, v in inputs.items()}
    arrays = dict(constants())
    arrays["x"] = i["x"].reshape(B * T, D)
    arrays["L0_attn_W_q"] = rows_on_partitions(i["L0_attn_W_q"])
    arrays["L0_attn_W_kv"] = rows_on_partitions(i["L0_attn_W_kv"])
    arrays["L0_attn_W_o"] = rows_on_partitions(i["L0_attn_W_o"].T)
    arrays["L0_xattn_Wq"] = rows_on_partitions(i["L0_xattn_Wq"].T)
    kv = np.concatenate([i["L0_xattn_Wk"], i["L0_xattn_Wv"]])
    arrays["L0_xattn_WK"] = rows_on_partitions(kv[0::2].T)
    arrays["L0_xattn_WV"] = rows_on_partitions(kv[1::2].T)
    arrays["ctxT"] = np.ascontiguousarray(i["ctx_2048"].transpose(0, 2, 1).reshape(B, C, P, S2).transpose(0, 2, 1, 3).reshape(B * P, C * S2))
    for n in ("1", "g", "2"):
        w = np.concatenate([i["L0_ffn_Ws" + n][None], i["L0_ffn_W" + n]])
        arrays["moe_W" + n] = np.concatenate([rows_on_partitions(a) for a in w])
    arrays["L0_ffn_gate_w"] = rows_on_partitions(i["L0_ffn_gate_w"])
    for n in ("L0_ffn_gate_b", "L0_ffn_biases"):
        arrays[n] = np.ascontiguousarray(np.broadcast_to(i[n], (T, ROUTED)))
    for n in "rkvgo":
        arrays["L1_attn_W_" + n] = rows_on_partitions(i["L1_attn_W_" + n].T)
    arrays["L1_attn_time_maa_w1"] = rows_on_partitions(i["L1_attn_time_maa_w1"])
    w2 = i["L1_attn_time_maa_w2"].reshape(5 * MIX, D)
    arrays["maa_w2"], arrays["maa_w2g"] = w2[:P], w2[P:]
    arrays["L1_attn_time_decay_w1"] = rows_on_partitions(i["L1_attn_time_decay_w1"])
    arrays["L1_attn_time_decay_w2"] = i["L1_attn_time_decay_w2"]
    per_feature = [i["L1_attn_time_maa_" + n] for n in "xwkvrg"] + [i["L1_attn_time_decay"], i["L1_attn_time_faaaa"]]
    arrays["rec_cols"] = np.concatenate([a.reshape(C, P).T for a in per_feature], 1)
    for n in ("L1_attn_ln_gamma", "L1_attn_ln_beta"):
        arrays[n] = np.broadcast_to(i[n], (T, D))
    arrays = {k: np.ascontiguousarray(a) for k, a in arrays.items()}
    for n in "qkvo":
        arrays["L1_xattn_W" + n] = rows_on_partitions(i["L1_xattn_W" + n].T)
    arrays["ma_bias_cols"] = np.concatenate([i["L1_xattn_b" + n].reshape(C, P).T for n in "qk"], 1)
    arrays["L1_xattn_bv"] = np.broadcast_to(i["L1_xattn_bv"], (P, D))
    for n in ("bo", "ln_gamma", "ln_beta"):
        arrays["L1_xattn_" + n] = np.broadcast_to(i["L1_xattn_" + n], (T, D))
    arrays["L1_xattn_residual_scale"] = np.broadcast_to(i["L1_xattn_residual_scale"], (T, 1))
    mask = np.zeros((B, 3, P), np.int32)
    for m, (at, n) in enumerate(CTX):
        mask[:, m, :n] = i["mask_BxS2_ik0"][:, at:at + n]
    arrays["mask_cols"] = mask.transpose(2, 0, 1).reshape(P, B * 3)
    arrays = {k: np.ascontiguousarray(a) for k, a in arrays.items()}
    for n in ("wq", "wk", "wv", "wo", "w_gate", "w_up", "w_down"):
        arrays["L1_ffn_" + n] = rows_on_partitions(i["L1_ffn_" + n])
    arrays["L1_ffn_w_router"] = np.broadcast_to(i["L1_ffn_w_router"], (T, D))
    arrays["rb_cols"] = np.concatenate([i["L1_ffn_" + n].reshape(-1, P).T for n in ("bq", "bk", "ln1_w")], 1)
    arrays["L1_ffn_bv"] = np.broadcast_to(i["L1_ffn_bv"], (HALF, 1024))
    arrays["L1_ffn_ln2_w"] = np.broadcast_to(i["L1_ffn_ln2_w"], (HALF, D))
    arrays = {k: np.ascontiguousarray(a) for k, a in arrays.items()}
    nc = _bacc.Bacc("TRN2", target_bir_lowering=False, num_devices=1)
    dram = {k: nc.dram_tensor(f"in_{k}", a.shape, mybir.dt.from_np(a.dtype), kind="ExternalInput").ap() for k, a in arrays.items()}
    out = nc.dram_tensor("out", (B, T, D), F32, kind="ExternalOutput").ap()
    build(nc, dram, out, STAGES)
    r = _run(nc, [{f"in_{k}": a for k, a in arrays.items()}], core_ids=[0])
    return r.results[0]["out"]
```
